# Optimizing a Trainium2 kernel written in Bass

```python
import numpy as np
import jax
import jax.numpy as jnp

def _softmax(x, axis=-1):
    return jax.nn.softmax(x, axis=axis)

def _gelu(x):
    return jax.nn.gelu(x, approximate=True)

def _silu(x):
    return jax.nn.silu(x)

def _sigmoid(x):
    return jax.nn.sigmoid(x)

def _layernorm(x, axis=-1, eps=1e-05):
    m = jnp.mean(x, axis=axis, keepdims=True)
    v = jnp.var(x, axis=axis, keepdims=True)
    return (x - m) / jnp.sqrt(v + eps)

def _scatter_add(tgt, idx, src, axis=0):
    return tgt.at[idx].add(src)

def _segment_sum(src, seg, n):
    return jax.ops.segment_sum(src, seg, n)
kernel_name = 'mk_prb_d1_jaxref_r4_728603'

def setup_inputs(seed: int=0):
    np.random.seed(seed)
    _w = jnp.asarray

    def _L0_attn_setup():
        import jax, jax.numpy as jnp
        import numpy as np
        BATCH, SEQ, DIM, DSTATE = (4, 512, 256, 32)
        key = jax.random.key(seed)
        ks = jax.random.split(key, 6)
        x = jax.random.normal(ks[0], (BATCH, SEQ, DIM), dtype=jnp.float32)
        log_A = jax.random.normal(ks[1], (DIM, DSTATE), dtype=jnp.float32) * 0.01 - 4.0
        B_w = jax.random.normal(ks[2], (DSTATE, DIM), dtype=jnp.float32) / np.sqrt(DIM)
        B_b = jnp.zeros((DSTATE,), jnp.float32)
        C_w = jax.random.normal(ks[3], (DSTATE, DIM), dtype=jnp.float32) / np.sqrt(DIM)
        C_b = jnp.zeros((DSTATE,), jnp.float32)
        D_skip = jnp.ones((DIM,), jnp.float32)
        dt_w = jax.random.normal(ks[4], (DIM, DIM), dtype=jnp.float32) / np.sqrt(DIM)
        dt_b = jnp.zeros((DIM,), jnp.float32)
        return dict(x=x, log_A=log_A, B_w=B_w, B_b=B_b, C_w=C_w, C_b=C_b, D_skip=D_skip, dt_w=dt_w, dt_b=dt_b)
    _L0_attn_in = _L0_attn_setup()

    def _L0_ffn_setup():
        import jax, jax.numpy as jnp
        import numpy as np
        B, S, D = (2, 512, 256)
        E, K, H = (8, 2, 1024)
        CAP_FACTOR = 1.0

        def _moe_forward(x, wg, w1, b1, w2, b2):
            Bb, Ss, Dd = x.shape
            T = Bb * Ss
            cap = int(K * CAP_FACTOR * ((T + E - 1) // E))
            xt = x.reshape(T, Dd)
            logits = xt @ wg
            scores = jax.nn.softmax(logits, axis=-1)
            gates_k, idx_k = jax.lax.top_k(scores, K)
            gates_k = gates_k / jnp.sum(gates_k, axis=-1, keepdims=True)
            masks = jax.nn.one_hot(idx_k, E, dtype=jnp.int32)
            m = jnp.transpose(masks, (1, 0, 2)).reshape(K * T, E)
            locs_full = jnp.cumsum(m, axis=0) - 1
            loc = jnp.sum(locs_full * m, axis=-1)
            loc = loc.reshape(K, T).T
            valid = (loc < cap).astype(xt.dtype)
            loc_c = jnp.clip(loc, 0, cap - 1)
            contrib = (xt[:, None, :] * valid[:, :, None]).reshape(T * K, Dd)
            disp = jnp.zeros((E, cap, Dd), xt.dtype)
            disp = disp.at[idx_k.reshape(-1), loc_c.reshape(-1)].add(contrib)
            h = jax.nn.relu(jnp.einsum('ecd,edh->ech', disp, w1) + b1[:, None, :])
            out = jnp.einsum('ech,ehd->ecd', h, w2) + b2[:, None, :]
            gathered = out[idx_k, loc_c]
            y = jnp.einsum('tk,tkd->td', gates_k * valid, gathered)
            return y.reshape(Bb, Ss, Dd)
        key = jax.random.key(seed)
        ks = jax.random.split(key, 6)
        scale_in = 1.0 / np.sqrt(D)
        scale_h = 1.0 / np.sqrt(H)
        return {'x': jax.random.normal(ks[0], (B, S, D), jnp.float32), 'wg': jax.random.normal(ks[1], (D, E), jnp.float32) * scale_in, 'w1': jax.random.normal(ks[2], (E, D, H), jnp.float32) * scale_in, 'b1': jnp.zeros((E, H), jnp.float32), 'w2': jax.random.normal(ks[3], (E, H, D), jnp.float32) * scale_h, 'b2': jnp.zeros((E, D), jnp.float32)}
    _L0_ffn_in = _L0_ffn_setup()
    _d = {'L0_attn_x': _L0_attn_in['x'], 'L0_attn_log_A': _L0_attn_in['log_A'], 'L0_attn_B_w': _L0_attn_in['B_w'], 'L0_attn_B_b': _L0_attn_in['B_b'], 'L0_attn_C_w': _L0_attn_in['C_w'], 'L0_attn_C_b': _L0_attn_in['C_b'], 'L0_attn_D_skip': _L0_attn_in['D_skip'], 'L0_attn_dt_w': _L0_attn_in['dt_w'], 'L0_attn_dt_b': _L0_attn_in['dt_b'], 'L0_ffn_wg': _L0_ffn_in['wg'], 'L0_ffn_w1': _L0_ffn_in['w1'], 'L0_ffn_b1': _L0_ffn_in['b1'], 'L0_ffn_w2': _L0_ffn_in['w2'], 'L0_ffn_b2': _L0_ffn_in['b2']}
    _x0 = _d['L0_attn_x']
    _d['L0_attn_x'] = jax.random.normal(jax.random.fold_in(jax.random.key(seed), 1), (16, 1024, 256), dtype=_x0.dtype)
    del _x0
    return _d

def reference(L0_attn_x, L0_attn_log_A, L0_attn_B_w, L0_attn_B_b, L0_attn_C_w, L0_attn_C_b, L0_attn_D_skip, L0_attn_dt_w, L0_attn_dt_b, L0_ffn_wg, L0_ffn_w1, L0_ffn_b1, L0_ffn_w2, L0_ffn_b2):

    def _L0_attn_ref(x, log_A, B_w, B_b, C_w, C_b, D_skip, dt_w, dt_b):
        import jax, jax.numpy as jnp
        import numpy as np
        BATCH, SEQ, DIM, DSTATE = (4, 512, 256, 32)
        Bsz, S, D = x.shape
        N = log_A.shape[1]
        dt = jax.nn.softplus(jnp.einsum('bsd,ed->bse', x, dt_w) + dt_b)
        A = -jnp.exp(log_A)
        b = jnp.einsum('bsd,nd->bsn', x, B_w) + B_b
        c = jnp.einsum('bsd,nd->bsn', x, C_w) + C_b

        def step(h, inp):
            x_t, dt_t, b_t, c_t = inp
            A_bar = jnp.exp(A[None] * dt_t[..., None])
            h = A_bar * h + (dt_t * x_t)[..., None] * b_t[:, None, :]
            y = jnp.einsum('bdn,bn->bd', h, c_t) + D_skip * x_t
            return (h, y)
        h0 = jnp.zeros((Bsz, D, N), x.dtype)
        xs = (jnp.swapaxes(x, 0, 1), jnp.swapaxes(dt, 0, 1), jnp.swapaxes(b, 0, 1), jnp.swapaxes(c, 0, 1))
        _, ys = jax.lax.scan(step, h0, xs)
        return jnp.swapaxes(ys, 0, 1)

    def _L0_ffn_ref(x, wg, w1, b1, w2, b2):
        import jax, jax.numpy as jnp
        import numpy as np
        B, S, D = (2, 512, 256)
        E, K, H = (8, 2, 1024)
        CAP_FACTOR = 1.0

        def _moe_forward(x, wg, w1, b1, w2, b2):
            Bb, Ss, Dd = x.shape
            T = Bb * Ss
            cap = int(K * CAP_FACTOR * ((T + E - 1) // E))
            xt = x.reshape(T, Dd)
            logits = xt @ wg
            scores = jax.nn.softmax(logits, axis=-1)
            gates_k, idx_k = jax.lax.top_k(scores, K)
            gates_k = gates_k / jnp.sum(gates_k, axis=-1, keepdims=True)
            masks = jax.nn.one_hot(idx_k, E, dtype=jnp.int32)
            m = jnp.transpose(masks, (1, 0, 2)).reshape(K * T, E)
            locs_full = jnp.cumsum(m, axis=0) - 1
            loc = jnp.sum(locs_full * m, axis=-1)
            loc = loc.reshape(K, T).T
            valid = (loc < cap).astype(xt.dtype)
            loc_c = jnp.clip(loc, 0, cap - 1)
            contrib = (xt[:, None, :] * valid[:, :, None]).reshape(T * K, Dd)
            disp = jnp.zeros((E, cap, Dd), xt.dtype)
            disp = disp.at[idx_k.reshape(-1), loc_c.reshape(-1)].add(contrib)
            h = jax.nn.relu(jnp.einsum('ecd,edh->ech', disp, w1) + b1[:, None, :])
            out = jnp.einsum('ech,ehd->ecd', h, w2) + b2[:, None, :]
            gathered = out[idx_k, loc_c]
            y = jnp.einsum('tk,tkd->td', gates_k * valid, gathered)
            return y.reshape(Bb, Ss, Dd)
        return _moe_forward(x, wg, w1, b1, w2, b2)
    x = L0_attn_x
    xn = _layernorm(x, axis=-1)
    x = x + _L0_attn_ref(xn, L0_attn_log_A, L0_attn_B_w, L0_attn_B_b, L0_attn_C_w, L0_attn_C_b, L0_attn_D_skip, L0_attn_dt_w, L0_attn_dt_b) + _L0_ffn_ref(xn, L0_ffn_wg, L0_ffn_w1, L0_ffn_b1, L0_ffn_w2, L0_ffn_b2)
    return x

_drawn_inputs = setup_inputs


def setup_inputs(seed=0):
    import zlib

    import numpy as np

    out = dict(_drawn_inputs(seed))
    spreads = {'L0_attn_B_b': (0.0, 0.1),
     'L0_attn_C_b': (0.0, 0.1),
     'L0_attn_D_skip': (1.0, 0.6),
     'L0_attn_dt_b': (0.0, 0.1),
     'L0_ffn_b1': (0.0, 0.8),
     'L0_ffn_b2': (0.0, 0.8)}
    factors = {'L0_attn_log_A': 7.488, 'L0_ffn_wg': 4.496, 'L0_ffn_w1': 4.809, 'L0_ffn_w2': 3.982}
    for name, (base, spread) in spreads.items():
        noise = np.random.default_rng([zlib.crc32(name.encode()), seed]).standard_normal(out[name].shape)
        drawn = base * np.exp(spread * noise) if base else spread * noise
        out[name] = jnp.asarray(drawn.astype(out[name].dtype))
    for name, factor in factors.items():
        out[name] = (out[name] * factor).astype(out[name].dtype)
    return out
```

```python
from contextlib import ExitStack

import concourse.bass as bass
from concourse import mybir

ALU = mybir.AluOpType
ACT = mybir.ActivationFunctionType
AX = mybir.AxisListType.X
F32 = mybir.dt.float32
BF16 = mybir.dt.bfloat16
I32 = mybir.dt.int32

P = 128
EPS = 1e-5


def ssm_moe(nc, x, log_a, bc_wt, bc_b, d_skip, dt_wt, dt_b, wg, w1, b1_t, w2, b2,
            ident_d, upper_d, emin_d, iota_d, tokval_d, sel_d, out):
    B, S, D = x.shape
    T = B * S
    N = log_a.shape[1] // 2
    E, _, H = w1.shape
    CAP = 2 * T // E
    NT = T // P
    KD = D // P
    HALF = S // 2
    TB = HALF // P
    NG = 8
    STEPS = B * 2 * (N // NG)
    SPE = STEPS // E
    HPE = SPE // (N // NG)
    G = 4
    NGRP = NT // G
    HC = H // P
    SL = 2 * T // STEPS
    SJ = SL // P
    Q = S // NG
    LPE = CAP // P
    BIG = float(1 << 20)

    xf = x.rearrange("b s d -> (b s) d")
    outf = out.rearrange("b s d -> (b s) d")
    xn_d = nc.dram_tensor("xn_rows", [T, D], F32, kind="Internal").ap()
    xnt_d = nc.dram_tensor("xn_transposed", [KD, P, T], F32, kind="Internal").ap()
    base_d = nc.dram_tensor("base_rows", [T, D], F32, kind="Internal").ap()
    y_d = nc.dram_tensor("scan_rows", [T, D], F32, kind="Internal").ap()
    y2_d = nc.dram_tensor("expert_rows", [2 * T, D], F32, kind="Internal").ap()
    b_d = nc.dram_tensor("b_rows", [2 * N, S], F32, kind="Internal").ap()

    def groups(a):
        return a.rearrange("(i j p) d -> i p j d", p=P, j=G)

    with ExitStack() as ctx:
        def sb(name, shape, dt=F32):
            return ctx.enter_context(nc.sbuf_tensor(name, shape, dt))

        def sem(name):
            return ctx.enter_context(nc.semaphore(name))

        bank = ctx.enter_context(nc.psum_tensor("bank", [P, 8, 512], F32))

        ident = sb("ident", [P, P])
        upper = sb("upper", [P, P])
        ones = sb("ones", [P, P])
        emin = sb("emin", [P, E])
        iota = sb("iota", [P, E * LPE])
        tokval = sb("tokval", [P, 2 * NT])
        sel = sb("sel", [96, N * P], BF16)
        ones3 = sb("ones3", [3, P], BF16)
        dskip = sb("dskip", [P, D])
        wg_sb = sb("wg_sb", [P, KD, E])
        a_neg = sb("a_neg", [P, KD * N])
        dtw = sb("dtw", [P, KD, D])
        dtb = sb("dtb", [P, KD])
        bcw = sb("bcw", [P, KD, P])
        bcb = sb("bcb", [P, 1])
        b1_sb = sb("b1_sb", [P, E * HC])
        b2_p = sb("b2_p", [3, E * D], BF16)
        w1_sb = sb("w1_sb", [P, KD, H])
        w2_sb = sb("w2_sb", [P, HC, D])
        h = sb("h", [P, 2 * NG, HALF])
        xt_in, xn, xbase, xnt_out = (h[:, 4 * i:4 * i + 4, :].rearrange("p (a b) t -> p a (b t)", a=2) for i in range(4))
        xt_in, xn, xbase = (t.rearrange("p a (j d) -> p a j d", d=D) for t in (xt_in, xn, xbase))
        xnt_out = xnt_out.rearrange("p a (k t) -> p a k t", k=KD)
        bstat = sb("bstat", [P, G, 6])
        mv = sb("mv", [P, 2, G, 2])
        rstd = sb("rstd", [P, 2, G])
        eps_c = sb("eps_c", [P, 1])
        b_sb = sb("b_sb", [P, 2, NG, HALF])
        logit, pos, oh0, oh1 = (b_sb[:, 1, 2 * i:2 * i + 2, :].rearrange("p a t -> p (a t)")
                                .rearrange("p (i e) -> p i e", e=E) for i in range(4))
        oh = [oh0, oh1]
        mx = [sb(f"mx{k}", [P, NT]) for k in range(2)]
        idx = [sb(f"idx{k}", [P, NT]) for k in range(2)]
        loc = [sb(f"loc{k}", [P, NT]) for k in range(2)]
        wk = [sb(f"wk{k}", [P, NT]) for k in range(2)]
        prt = sb("prt", [P, 2, NT])
        col = sb("col", [P, 2, NT])
        tmp_i = sb("tmp_i", [P, NT], I32)
        tmp_i2 = sb("tmp_i2", [P, NT], I32)
        u = sb("u", [P, 4, HALF])
        u_flat = u[:].rearrange("p a t -> p (a t)")
        oh_p = u_flat[:, 0:4 * P].rearrange("p (r c) -> p r c", r=4)
        oh_c = u_flat[:, 4 * P:4 * P + 4 * E * LPE].rearrange("p (r c) -> p r c", r=4)
        map_f = sb("map_f", [P, E * LPE])
        map_g = sb("map_g", [P, E * LPE])
        slot_dst = sb("slot_dst", [P, SJ + E * LPE + SJ], I32)
        slot_tok = sb("slot_tok", [P, SJ + E * LPE + SJ], I32)
        hc = sb("hc", [P, 4, HALF])
        zeros = hc[:].rearrange("p a t -> p (a t)")
        xnt = sb("xnt", [P, 2, KD, S])
        dt = sb("dt", [P, 2, KD, S])
        dtx = sb("dtx", [P, 2, KD, S])
        c_p = sb("c_p", [96, 2, S], BF16)
        carry = sb("carry", [P, 2, KD * N])
        base_sb = sb("base_sb", [P, TB, D])
        y_sb = sb("y_sb", [P, TB, D])
        b2_f = dt[0:3, 1].rearrange("p k t -> p (k t)")
        b2_r = dtx[0:3, 1].rearrange("p k t -> p (k t)")
        b2_q = y_sb[0:3].rearrange("p j d -> p (j d)").bitcast(BF16)
        za = sb("za", [P, KD, Q])
        zr = sb("zr", [P, KD, Q])
        ze = sb("ze", [P, KD, Q])
        zl = sb("zl", [P, KD, Q])
        bcv = sb("bcv", [P, Q])
        c_r = sb("c_r", [96, Q])
        gidx = sb("gidx", [P, SJ], I32)
        sidx = sb("sidx", [P, SJ], I32)
        xg = sb("xg", [P, SJ, D])
        xgt = sb("xgt", [P, KD, SL])
        ht = sb("ht", [P, HC, SL])
        o_sb = sb("o_sb", [P, SJ, D])

        y_ps = bank[:, 0:2, :]
        y_blk = y_ps.rearrange("p b (t d) -> p (b t) d", d=D)
        a_ps = [bank[:, 2, :], bank[:, 3, :]]
        c_ps = bank[:, 4, :]
        m_ps = [bank[:, 5, :], bank[:, 6, :]]

        waits_passed = sem("waits_passed")
        consts_in = sem("consts_in")
        weights_in = sem("weights_in")
        x_in = [sem(f"x_in{i}") for i in range(2)]
        stats_done = sem("stats_done")
        aggr_done = sem("aggr_done")
        std_done = sem("std_done")
        rstd_done = sem("rstd_done")
        xn_done = sem("xn_done")
        xn_out = [sem(f"xn_out{i}") for i in range(2)]
        xnt_st = [sem(f"xnt_st{i}") for i in range(2)]
        base_out = [sem(f"base_out{i}") for i in range(2)]
        skip_done = sem("skip_done")
        base_done = sem("base_done")
        turned = sem("turned")
        xnt_done = sem("xnt_done")
        logits_done = sem("logits_done")
        dve_seq = sem("dve_seq")
        pe_route = sem("pe_route")
        gate_in = sem("gate_in")
        gate_out = sem("gate_out")
        oh_ready = sem("oh_ready")
        oh_used = sem("oh_used")
        map_ready = sem("map_ready")
        zero_rows = sem("zero_rows")
        setup_act = sem("setup_act")
        setup_dve = sem("setup_dve")
        xnt_in = sem("xnt_in")
        b_in = sem("b_in")
        b_st = sem("b_st")
        base_in = sem("base_in")
        w1_in = sem("w1_in")
        w2_in = sem("w2_in")
        xg_in = sem("xg_in")
        gidx_done = sem("gidx_done")
        sidx_done = sem("sidx_done")
        o_scattered = sem("o_scattered")
        fill_done = sem("fill_done")
        evac_done = sem("evac_done")
        c_ready = sem("c_ready")
        a_ready = sem("a_ready")
        u_ready = sem("u_ready")
        scan_done = sem("scan_done")
        hc_done = sem("hc_done")
        nsum_done = sem("nsum_done")
        carry_done = sem("carry_done")
        base_added = sem("base_added")
        y_evac = sem("y_evac")
        y_out = sem("y_out")
        z_done = sem("z_done")
        v_done = sem("v_done")
        l_done = sem("l_done")
        dt_done = sem("dt_done")
        r1_done = sem("r1_done")
        r2_done = sem("r2_done")
        c2_done = sem("c2_done")
        c_parts = sem("c_parts")
        prep_done = sem("prep_done")
        fin_in = [sem(f"fin_in{i}") for i in range(2)]
        fin_mid = sem("fin_mid")
        fin_done = sem("fin_done")
        fin_out = [sem(f"fin_out{i}") for i in range(2)]

        FP = NG
        FS = 2 + HC // 2 + SJ
        SCAN0, NSUM0 = 4, 2

        def settle(eng):
            eng.sem_inc(waits_passed, 1)

        def start_at_one(eng, *sems):
            for s in sems:
                eng.sem_inc(s, 1)

        def moe_pieces():
            out = [(0, 0.43, "turn", None), (1, 1.28, "prep", None)]
            for f in range(HC // 2):
                out += [(2 + f, 0.85, "up", (f, c)) for c in range(2)]
            for j in range(SJ):
                out += [(2 + HC // 2 + j, 0.43, "down", (j, hh)) for hh in range(HC)]
                out += [(2 + HC // 2 + j, 0.1, "bias", j)]
            return out

        pieces = moe_pieces()
        total = sum(c for _, c, _, _ in pieces)
        share = [total / (NG - 0.55)] * (NG - 1) + [total]
        slices, at, acc = [], 0, 0.0
        for k in range(NG):
            acc += share[k]
            take = []
            while at < len(pieces) and sum(c for _, c, _, _ in pieces[:at + 1]) <= acc + 0.25:
                take.append(pieces[at])
                at += 1
            slices.append(take)
        slices[-1] += pieces[at:]
        last_of = {}
        for k, take in enumerate(slices):
            for piece in take:
                last_of[piece[0]] = k
        evac_at = {f: min(last_of[f] + 1, NG - 1) for f in last_of}

        block = ctx.enter_context(nc.Block())

        @block.sync
        def _(sp):
            start_at_one(sp, *xn_out, *base_out, b_st, *fin_out)
            for dst, src in ((ident, ident_d), (upper, upper_d), (emin, emin_d), (iota, iota_d),
                             (tokval, tokval_d), (sel, sel_d), (dskip, d_skip.partition_broadcast(P)),
                             (wg_sb, wg.rearrange("(k p) e -> p k e", p=P))):
                sp.dma_start(dst[:], src).then_inc(consts_in, 16)
            x_g, xn_g, base_g, y_g = groups(xf), groups(xn_d), groups(base_d), groups(y_d)

            def load_x(par, grp):
                sp.dma_start(xt_in[:, par], x_g[bass.ds(grp, 1)].rearrange("a p j d -> (a p) j d")).then_inc(x_in[par], 16)

            for par in range(2):
                load_x(par, par)
            for dst, src in ((a_neg, log_a), (dtw, dt_wt.rearrange("(k p) e -> p k e", p=P)), (dtb, dt_b),
                             (bcw, bc_wt.rearrange("(k p) e -> p k e", p=P)), (bcb, bc_b),
                             (b1_sb, b1_t), (b2_f, b2.partition_broadcast(3))):
                sp.dma_start(dst if dst is b2_f else dst[:], src).then_inc(weights_in, 16)

            with sp.Fori(0, NGRP // 2) as ii:
                for par in range(2):
                    sp.wait_ge(xn_done, ii * 2 + par + 2)
                    sp.dma_start(xn_g[bass.ds(ii * 2 + par, 1)].rearrange("a p j d -> (a p) j d"),
                                 xn[:, par]).then_inc(xn_out[par], 16)
                    sp.wait_ge(base_done, ii * 2 + par + 1)
                    sp.dma_start(base_g[bass.ds(ii * 2 + par, 1)].rearrange("a p j d -> (a p) j d"),
                                 xbase[:, par]).then_inc(base_out[par], 16)
                    sp.wait_ge(stats_done, ii * 2 + par + 1)
                    load_x(par, (ii * 2 + par + 2) % NGRP)
            for par in range(2):
                sp.wait_ge(xnt_st[par], 16 * (NGRP // 2) + 1)
                sp.wait_ge(xn_out[par], 16 * (NGRP // 2) + 1)
                sp.wait_ge(base_out[par], 16 * (NGRP // 2) + 1)
                sp.wait_ge(x_in[par], 16 * (NGRP // 2 + 1))

            def load_xnt(par, b):
                src = xnt_d.rearrange("k p t -> p k t")[:, :, bass.ds(b * S, S)]
                sp.dma_start(xnt[:, par], src).then_inc(xnt_in, 16)

            def load_base(hf):
                src = base_g[bass.ds(hf, 1)].rearrange("a p j d -> (a p) j d")
                sp.dma_start(base_sb[:], src).then_inc(base_in, 16)

            def load_w1(e):
                src = w1[bass.ds(e, 1)].rearrange("a (k p) h -> p (a k) h", p=P)
                sp.dma_start(w1_sb[:], src).then_inc(w1_in, 16)

            def load_w2(e):
                src = w2[bass.ds(e, 1)].rearrange("a (c p) d -> p (a c) d", p=P)
                sp.dma_start(w2_sb[:], src).then_inc(w2_in, 16)

            def load_b(buf, par, th, ng):
                src = b_d[bass.ds(par * N + ng * NG, NG), bass.ds(th * HALF, HALF)].partition_broadcast(P)
                dst = b_sb[:, bass.ds(buf, 1)].rearrange("p a n t -> p (a n) t")
                sp.dma_start(dst, src).then_inc(b_in, 16)

            load_xnt(0, 0)
            sp.wait_ge(xnt_in, 16)
            load_xnt(1, 1)
            load_base(0)
            load_w1(0)
            load_w2(0)
            with sp.Fori(0, NG) as q:
                sp.wait_ge(evac_done, q + 2)
                sp.dma_start(b_d[0:N, bass.ds(q * Q, Q)], bcv[96:P, :]).then_inc(b_st, 16)
            sp.wait_ge(setup_act, 1)
            y2_z = y2_d.rearrange("(i p r) d -> i p (r d)", p=P, r=8)
            with sp.Fori(0, 2 * T // (P * 8)) as i:
                sp.dma_start(y2_z[bass.ds(i, 1)].rearrange("a p r -> (a p) r"), zeros).then_inc(zero_rows, 16)
            sp.wait_ge(b_st, 16 * NG + 1)
            sp.wait_ge(prep_done, NG + 1)
            sp.wait_ge(xnt_in, 32)
            load_xnt(0, 2)
            load_b(0, 0, 0, 0)
            sp.wait_ge(map_ready, 1)

            with sp.Fori(0, E) as e:
                with sp.Fori(0, HPE) as hh:
                    with sp.Fori(0, N // NG) as ng:
                        st = e * SPE + hh * (N // NG) + ng
                        nx = st + 1
                        sp.wait_ge(u_ready, st * 2 * NG + 1)
                        sp.wait_ge(b_in, 16 * (st + 1))
                        sp.wait_ge(b_st, 16 * (NG + st) + 1)
                        load_b(nx % 2, (nx // NG) % 2, (nx // (N // NG)) % 2, nx % (N // NG))
                        sp.wait_ge(evac_done, FP + st * FS + 2 + 1)
                        settle(sp)
                        sp.dma_start(b_d[bass.ds((1 - hh // 2) * N, N), bass.ds(((hh % 2) * (N // NG) + ng) * Q, Q)],
                                     bcv[96:P, :]).then_inc(b_st, 16)
                    hf = e * HPE + hh
                    sp.wait_ge(base_added, hf + 1)
                    load_base((hf + 1) % (2 * B))
                    sp.wait_ge(prep_done, FP + (hf + 1) * (N // NG) + 1)
                    sp.wait_ge(xnt_in, 16 * (hf + 3))
                    settle(sp)
                    src = xnt_d.rearrange("k p t -> p k t")[:, :, bass.ds((hf // 2 + 3) % B * S + hh % 2 * HALF, HALF)]
                    sp.dma_start(xnt[:, bass.ds(1 - hh // 2, 1), :, bass.ds(hh % 2 * HALF, HALF)]
                                 .rearrange("p a k t -> p (a k) t"), src).then_inc(xnt_in, 16)
                last = FP + (e + 1) * SPE * FS
                sp.wait_ge(fill_done, last - SJ)
                load_w1((e + 1) % E)
                sp.wait_ge(fill_done, last)
                load_w2((e + 1) % E)
            sp.wait_ge(w1_in, 16 * (E + 1))
            sp.wait_ge(w2_in, 16 * (E + 1))
            sp.wait_ge(b_in, 16 * (STEPS + 1))
            sp.wait_ge(b_st, 16 * (NG + STEPS) + 1)
            sp.wait_ge(base_in, 16 * (2 * B + 1))
            sp.wait_ge(xnt_in, 16 * (2 * B + 3))

            sp.wait_ge(y_out, 16 * 2 * B + 1)
            sp.wait_ge(o_scattered, 16 * SJ * (STEPS + 1))
            y2_g = y2_d.rearrange("(k i j p) d -> k i p j d", p=P, j=G, k=2)
            out_g = groups(outf)
            sp.wait_ge(c_parts, NG + STEPS + 1)
            sp.wait_ge(carry_done, STEPS + 1)

            def fin_load(par, grp):
                sp.dma_start(xn[:, par], y_g[bass.ds(grp, 1)].rearrange("a p j d -> (a p) j d")).then_inc(fin_in[par], 16)
                for k, dst in enumerate((xt_in, xbase)):
                    sp.dma_start(dst[:, par], y2_g[k, bass.ds(grp, 1)].rearrange("a p j d -> (a p) j d")
                                 ).then_inc(fin_in[par], 16)

            for par in range(2):
                fin_load(par, par)
            with sp.Fori(0, NGRP // 2) as ii:
                for par in range(2):
                    sp.wait_ge(fin_done, (ii * 2 + par + 1) * G + 1)
                    sp.dma_start(out_g[bass.ds(ii * 2 + par, 1)].rearrange("a p j d -> (a p) j d"),
                                 xnt_out[:, par].rearrange("p k (j d) -> p (k j) d", d=D)).then_inc(fin_out[par], 16)
                    fin_load(par, (ii * 2 + par + 2) % NGRP)
            for par in range(2):
                sp.wait_ge(fin_out[par], 16 * (NGRP // 2) + 1)
                sp.wait_ge(fin_in[par], 48 * (NGRP // 2 + 1))

        @block.tensor
        def _(pe):
            def turn(dst, src, start):
                return pe.matmul(dst, src, ident[:], start=start, stop=True, is_transpose=True, skip_group_check=True)

            start_at_one(pe, turned, logits_done, c_ready)
            pe.wait_ge(consts_in, 16 * 8)
            lg_ps = bank[:, 4:6, :].rearrange("p b c -> p (b c)")
            with pe.Fori(0, NGRP // 2) as ii:
                for par in range(2):
                    pe.wait_ge(xn_done, ii * 2 + par + 2)
                    pe.wait_ge(xnt_done, ii * 2 + par + 1)
                    for k in range(KD):
                        for j in range(G):
                            mm = turn(bank[:, 2 * par + k, j * P:(j + 1) * P], xn[:, par, j, k * P:(k + 1) * P], True)
                    mm.then_inc(turned, 1)
                    pe.wait_ge(xnt_done, ii * 2 + par + 2)
                    for j in range(G):
                        for k in range(KD):
                            mm = pe.matmul(lg_ps[:, bass.ds((ii * 2 + par) * G * E + j * E, E)],
                                           xnt_out[:, par, k, j * P:(j + 1) * P], wg_sb[:, k, :],
                                           start=(k == 0), stop=(k == KD - 1))
                    mm.then_inc(logits_done, 1)

            for k in range(2):
                pe.wait_ge(gate_in, k + 1)
                ohf = oh[k].rearrange("p i e -> p (i e)")
                for c in range(2):
                    pe.matmul(bank[:, c, :], upper[:], ohf[:, c * 512:(c + 1) * 512], start=True, stop=True)
                    mm = pe.matmul(bank[:, 2 + c, :], ones[:], ohf[:, c * 512:(c + 1) * 512], start=True, stop=True)
                mm.then_inc(pe_route, 1)
                pe.wait_ge(gate_out, k + 1)
            pe.wait_ge(setup_dve, 1)
            with pe.Fori(0, 2 * NT // 4) as i:
                for r in range(4):
                    pe.wait_ge(oh_ready, i * 4 + r + 1)
                    pe.matmul(bank[:, 7, 0:E * LPE], oh_p[:, r, :], oh_c[:, r, :], start=False, stop=True,
                              skip_group_check=True).then_inc(oh_used, 1)

            def prep(par, q, f):
                for g in range(3):
                    w = dtw[:, :, g * P:(g + 1) * P] if g < 2 else bcw[:]
                    for k in range(KD):
                        src = xnt[:, bass.ds(par, 1), k, bass.ds(q * Q, Q)].rearrange("p a t -> p (a t)")
                        mm = pe.matmul(m_ps[f][:, g * Q:(g + 1) * Q], w[:, k, :], src, start=(k == 0), stop=(k == KD - 1))
                return mm

            pe.wait_ge(weights_in, 16 * 7)
            pe.wait_ge(xnt_in, 16)
            with pe.Fori(0, NG // 2) as i:
                for f in range(2):
                    pe.wait_ge(evac_done, i * 2 + f + 1)
                    prep(0, i * 2 + f, f).then_inc(fill_done, 1)
            pe.sem_inc(nsum_done, NSUM0)

            with pe.Fori(0, E) as e:
                with pe.Fori(0, HPE) as hh:
                    hf = e * HPE + hh
                    pe.wait_ge(base_in, 16 * (hf + 1))
                    pe.wait_ge(y_evac, hf + 1)
                    for c in range(2):
                        mm = pe.matmul(y_ps[:, c, :], ident[:],
                                       base_sb[:, 2 * c:2 * c + 2, :].rearrange("p j d -> p (j d)"),
                                       start=True, stop=True, skip_group_check=True)
                    mm.then_inc(base_added, 1)
                    pe.wait_ge(c_parts, (hf + 1) * (N // NG) + 1)
                    settle(pe)
                    with pe.Fori(0, N // NG) as ng:
                        st = hf * (N // NG) + ng
                        for k in range(NG):
                            pe.wait_ge(hc_done, st * 2 * NG + 2 * k + 1)
                            pe.matmul(c_ps, sel[:, bass.ds(ng * NG * P + k * P, P)],
                                      c_p[:, bass.ds(hh // 2, 1), bass.ds((hh % 2) * HALF, HALF)]
                                      .rearrange("p a t -> p (a t)"), start=True, stop=True).then_inc(c_ready, 1)
                            for n, (f, _, kind, arg) in enumerate(slices[k]):
                                starts = pieces.index(slices[k][n]) == [p[0] for p in pieces].index(f)
                                ends = pieces.index(slices[k][n]) == max(i for i, p in enumerate(pieces) if p[0] == f)
                                m = m_ps[f % 2]
                                if starts:
                                    pe.wait_ge(evac_done, FP + st * FS + f - 1 + 1)
                                if kind == "turn":
                                    pe.wait_ge(xg_in, 16 * SJ * (st + 1))
                                    for kk in range(KD):
                                        for j in range(SJ):
                                            mm = turn(m[:, kk * SL + j * P:kk * SL + (j + 1) * P],
                                                      xg[:, j, kk * P:(kk + 1) * P], True)
                                elif kind == "prep":
                                    pe.wait_ge(xnt_in, 16 * (hf // 2 * 2 + 2))
                                    settle(pe)
                                    mm = prep(1 - hh // 2, (hh % 2) * (N // NG) + ng, f % 2)
                                elif kind == "up":
                                    if arg == (0, 0):
                                        pe.wait_ge(w1_in, 16 * (e + 1))
                                        pe.wait_ge(evac_done, FP + st * FS + 2)
                                    ch = 2 * arg[0] + arg[1]
                                    for kk in range(KD):
                                        mm = pe.matmul(m[:, arg[1] * SL:(arg[1] + 1) * SL],
                                                       w1_sb[:, kk, ch * P:(ch + 1) * P], xgt[:, kk, :],
                                                       start=(kk == 0), stop=(kk == KD - 1))
                                elif kind == "down":
                                    j, c = arg
                                    if c == 0:
                                        pe.wait_ge(w2_in, 16 * (e + 1))
                                    if j == 0 and c % 2 == 0:
                                        pe.wait_ge(evac_done, FP + st * FS + 2 + c // 2 + 2)
                                    mm = pe.matmul(m[:, 0:D], ht[:, c, j * P:(j + 1) * P], w2_sb[:, c, :],
                                                   start=(c == 0), stop=False)
                                else:
                                    mm = pe.matmul(m[:, 0:D], ones3[:], b2_p[:, bass.ds(e * D, D)],
                                                   start=False, stop=True)
                                if ends:
                                    mm.then_inc(fill_done, 1)
                            for dh in range(KD):
                                pe.wait_ge(hc_done, st * 2 * NG + 2 * k + dh + 2)
                                for tb in range(TB):
                                    mm = turn(y_blk[:, tb, dh * P:(dh + 1) * P],
                                              hc[:, (2 * k + dh) % 4, tb * P:(tb + 1) * P], False)
                            mm.then_inc(nsum_done, 1)

        @block.scalar
        def _(act):
            start_at_one(act, *xnt_st, xnt_done, evac_done, a_ready, y_evac, y_out, c_parts)
            act.wait_ge(setup_dve, 1)
            act.wait_ge(aggr_done, 1)

            def std(par):
                return act.activation(rstd[:, par, :], mv[:, par, :, 1], ACT.Sqrt, bias=eps_c[:, 0:1])

            xnt_g = xnt_d.rearrange("k p (i t) -> i p k t", t=G * P)
            std(0).then_inc(std_done, 1)
            with act.Fori(0, NGRP // 2) as ii:
                for par in range(2):
                    act.wait_ge(aggr_done, ii * 2 + par + 2)
                    act.wait_ge(xn_done, ii * 2 + par + 1)
                    std(1 - par).then_inc(std_done, 1)
                    act.wait_ge(turned, ii * 2 + par + 2)
                    act.wait_ge(xnt_st[par], 16 * ii + 1)
                    act.wait_ge(logits_done, ii * 2 + 1)
                    act.activation(xnt_out[:, par].rearrange("p k t -> p (k t)"),
                                   bank[:, 2 * par:2 * par + 2, :].rearrange("p b c -> p (b c)"),
                                   ACT.Copy).then_inc(xnt_done, 1)
                    act.wait_ge(xnt_done, ii * 2 + par + 2)
                    act.dma_start(xnt_g[bass.ds(ii * 2 + par, 1)].rearrange("a p k t -> (a p) k t"),
                                  xnt_out[:, par]).then_inc(xnt_st[par], 16)

            act.preload_act_table_set("natural_log_exp_and_others")
            act.wait_ge(weights_in, 16 * 7)
            act.activation(a_neg[:], a_neg[:], ACT.Exp).then_inc(setup_act, 1)
            act.wait_ge(setup_act, 1)
            act.mul(a_neg[:], a_neg[:], -1.0).then_inc(setup_act, 1)
            act.wait_ge(gate_in, 3)
            act.activation(wk[1][:], wk[1][:], ACT.Exp).then_inc(setup_act, 1)
            act.wait_ge(setup_act, 3)

            def evac_prep(m, pdone, par, q):
                for g in range(KD):
                    act.activation(za[:, g, :], m[:, g * Q:(g + 1) * Q], ACT.Abs, bias=dtb[:, g:g + 1])
                for g in range(KD):
                    ins = act.activation(zr[:, g, :], m[:, g * Q:(g + 1) * Q], ACT.Relu, bias=dtb[:, g:g + 1])
                ins.then_inc(z_done, 1)
                act.wait_ge(b_st, 16 * pdone + 1)
                act.activation(bcv[:], m[:, 2 * Q:3 * Q], ACT.Identity, bias=bcb[:, 0:1]).then_inc(evac_done, 1)
                act.wait_ge(z_done, pdone + 1)
                act.activation(ze[:], za[:], ACT.Exp, scale=-1.0).then_inc(v_done, 1)
                act.wait_ge(v_done, pdone + 1)
                c1 = c_p[:, bass.ds(par, 1), bass.ds(q * Q, Q)].rearrange("p a t -> p (a t)")
                act.activation(c1, bcv[0:96, :], ACT.Copy)
                act.activation(zl[:], ze[:], ACT.Ln, bias=1.0).then_inc(l_done, 1)

            def c_part2(pdone, par, q):
                act.wait_ge(r1_done, pdone + 1)
                settle(act)
                for r in (32, 64):
                    ins = act.activation(c_p[r:r + 32, bass.ds(par, 1), bass.ds(q * Q, Q)].rearrange("p a t -> p (a t)"),
                                         c_r[r:r + 32, :], ACT.Copy)
                ins.then_inc(c2_done, 1)

            def c_part3(pdone, par, q):
                act.wait_ge(r2_done, pdone + 1)
                settle(act)
                act.activation(c_p[64:96, bass.ds(par, 1), bass.ds(q * Q, Q)].rearrange("p a t -> p (a t)"),
                               c_r[64:96, :], ACT.Copy).then_inc(c_parts, 1)

            with act.Fori(0, NG // 2) as i:
                for f in range(2):
                    act.wait_ge(fill_done, i * 2 + f + 1)
                    act.wait_ge(prep_done, i * 2 + f + 1)
                    evac_prep(m_ps[f], i * 2 + f, 0, i * 2 + f)
                    c_part2(i * 2 + f, 0, i * 2 + f)
                    c_part3(i * 2 + f, 0, i * 2 + f)

            with act.Fori(0, E) as e:
                with act.Fori(0, HPE) as hh:
                    hf = e * HPE + hh
                    act.wait_ge(prep_done, (hf + 1) * (N // NG) + 1)
                    with act.Fori(0, N // NG) as ng:
                        st = hf * (N // NG) + ng
                        for k in range(NG):
                            for dh in range(KD):
                                act.wait_ge(scan_done, st * 2 * NG + 2 * k + dh - 1 + SCAN0)
                                act.activation(a_ps[dh],
                                               dt[:, bass.ds(hh // 2, 1), dh, bass.ds((hh % 2) * HALF, HALF)]
                                               .rearrange("p a t -> p (a t)"), ACT.Exp,
                                               scale=a_neg[:, bass.ds(dh * N + ng * NG + k, 1)]).then_inc(a_ready, 1)
                            for f in sorted(evac_at):
                                if evac_at[f] != k:
                                    continue
                                m = m_ps[f % 2]
                                act.wait_ge(fill_done, FP + st * FS + f + 1)
                                if f == 0:
                                    act.activation(xgt[:].rearrange("p k s -> p (k s)"), m,
                                                   ACT.Copy).then_inc(evac_done, 1)
                                elif f == 1:
                                    act.wait_ge(prep_done, FP + st + 1)
                                    evac_prep(m, FP + st, 1 - hh // 2, (hh % 2) * (N // NG) + ng)
                                elif f < 2 + HC // 2:
                                    for c in range(2):
                                        ch = 2 * (f - 2) + c
                                        ins = act.activation(ht[:, ch, :], m[:, c * SL:(c + 1) * SL], ACT.Relu,
                                                             bias=b1_sb[:, bass.ds(e * HC + ch, 1)])
                                    ins.then_inc(evac_done, 1)
                                else:
                                    j = f - 2 - HC // 2
                                    if j == 0:
                                        act.wait_ge(o_scattered, 16 * SJ * (st + 1))
                                    act.activation(o_sb[:, j, :], m[:, 0:D], ACT.Copy).then_inc(evac_done, 1)
                            if k == 5:
                                c_part2(FP + st, 1 - hh // 2, (hh % 2) * (N // NG) + ng)
                            if k == 7:
                                c_part3(FP + st, 1 - hh // 2, (hh % 2) * (N // NG) + ng)
                    act.wait_ge(nsum_done, (hf + 1) * N + NSUM0)
                    act.wait_ge(y_out, 16 * hf + 1)
                    act.activation(y_sb[:].rearrange("p j d -> p (j d)"), y_ps.rearrange("p b c -> p (b c)"),
                                   ACT.Copy).then_inc(y_evac, 1)
                    act.wait_ge(y_evac, hf + 2)
                    act.dma_start(groups(y_d)[bass.ds(hf, 1)].rearrange("a p j d -> (a p) j d"),
                                  y_sb[:]).then_inc(y_out, 16)

        @block.gpsimd
        def _(pool):
            start_at_one(pool, skip_done, prep_done, u_ready)
            pool.wait_ge(consts_in, 16 * 8)
            dsk = dskip[:].unsqueeze(1).to_broadcast([P, G, D])
            with pool.Fori(0, NGRP // 2) as ii:
                for par in range(2):
                    pool.wait_ge(xn_done, ii * 2 + par + 2)
                    pool.wait_ge(base_out[par], 16 * ii + 1)
                    pool.tensor_tensor(xbase[:, par], xn[:, par], dsk, ALU.mult).then_inc(skip_done, 1)
                    pool.wait_ge(skip_done, ii * 2 + par + 2)
                    pool.tensor_tensor(xbase[:, par], xbase[:, par], xt_in[:, par], ALU.add).then_inc(base_done, 1)

            def prep(pdone, par, q):
                dst = lambda t: t[:, bass.ds(par, 1), :, bass.ds(q * Q, Q)].rearrange("p a k t -> p (a k) t")
                pool.wait_ge(l_done, pdone + 1)
                settle(pool)
                pool.tensor_tensor(dst(dt), zr[:], zl[:], ALU.add).then_inc(dt_done, 1)
                pool.wait_ge(c_parts, pdone + 1)
                settle(pool)
                c_all = c_p[:, bass.ds(par, 1), bass.ds(q * Q, Q)].rearrange("p a t -> p (a t)")
                pool.tensor_tensor(c_r[:], bcv[0:96, :], c_all, ALU.subtract).then_inc(r1_done, 1)
                pool.wait_ge(dt_done, pdone + 1)
                settle(pool)
                pool.tensor_tensor(dst(dtx), dst(dt), dst(xnt), ALU.mult).then_inc(prep_done, 1)

            def prep_c(pdone, par, q):
                pool.wait_ge(c2_done, pdone + 1)
                settle(pool)
                c_all = c_p[:, bass.ds(par, 1), bass.ds(q * Q, Q)].rearrange("p a t -> p (a t)")
                pool.tensor_tensor(c_r[:], c_r[:], c_all, ALU.subtract).then_inc(r2_done, 1)

            def gather(st, nx):
                pool.tensor_copy(gidx[:], slot_tok[:, bass.ds(nx * SJ + SJ, SJ)]).then_inc(gidx_done, 1)
                pool.wait_ge(gidx_done, nx + 1)
                settle(pool)
                for j in range(SJ):
                    pool.indirect_dma_start(xg[:, j, :], None, xn_d, bass.IndirectOffsetOnAxis(ap=gidx[:, j:j + 1], axis=0),
                                            bounds_check=T - 1, oob_is_err=False).then_inc(xg_in, 16)

            def scatter(st):
                pool.tensor_copy(sidx[:], slot_dst[:, bass.ds(st * SJ, SJ)]).then_inc(sidx_done, 1)
                pool.wait_ge(sidx_done, st + 1)
                settle(pool)
                for j in range(SJ):
                    pool.indirect_dma_start(y2_d, bass.IndirectOffsetOnAxis(ap=sidx[:, j:j + 1], axis=0), o_sb[:, j, :], None,
                                            bounds_check=2 * T - 1, oob_is_err=False).then_inc(o_scattered, 16)

            with pool.Fori(0, NG) as q:
                prep(q, 0, q)
                prep_c(q, 0, q)
            pool.wait_ge(map_ready, 1)
            pool.wait_ge(xn_out[0], 16 * (NGRP // 2) + 1)
            pool.wait_ge(xn_out[1], 16 * (NGRP // 2) + 1)
            gather(0, 0)
            pool.wait_ge(zero_rows, 16 * (2 * T // (P * 8)))

            with pool.Fori(0, E) as e:
                with pool.Fori(0, HPE) as hh:
                    hf = e * HPE + hh
                    with pool.Fori(0, N // NG) as ng:
                        st = hf * (N // NG) + ng
                        pool.wait_ge(b_in, 16 * (st + 1))
                        for k in range(NG):
                            for dh in range(KD):
                                p = 2 * k + dh
                                pool.wait_ge(scan_done, st * 2 * NG + p - 3 + SCAN0)
                                settle(pool)
                                pool.tensor_tensor(u[:, p % 4, :],
                                                   dtx[:, bass.ds(hh // 2, 1), dh, bass.ds((hh % 2) * HALF, HALF)]
                                                   .rearrange("p a t -> p (a t)"),
                                                   b_sb[:, bass.ds(st % 2, 1), k, :].rearrange("p a t -> p (a t)"),
                                                   ALU.mult).then_inc(u_ready, 1)
                            if k == 1:
                                pool.wait_ge(evac_done, FP + st * FS + 1)
                                scatter(st)
                            if k == 2:
                                pool.wait_ge(fill_done, FP + st * FS + 1)
                                gather(st, st + 1)
                            if k == 4:
                                pool.wait_ge(c_ready, (hf // 2) * 2 * N + 1)
                                pool.wait_ge(a_ready, (hf // 2) * 4 * N + 1)
                                prep(FP + st, 1 - hh // 2, (hh % 2) * (N // NG) + ng)
                            if k == 6:
                                prep_c(FP + st, 1 - hh // 2, (hh % 2) * (N // NG) + ng)
            pool.wait_ge(evac_done, FP + STEPS * FS + 1)
            scatter(STEPS)
            pool.wait_ge(o_scattered, 16 * SJ * (STEPS + 1))
            pool.wait_ge(xg_in, 16 * SJ * (STEPS + 1))

        @block.vector
        def _(dve):
            start_at_one(dve, xn_done, hc_done, carry_done, fin_done)
            seq = [0]

            def link(ins):
                seq[0] += 1
                ins.then_inc(dve_seq, 1)
                dve.wait_ge(dve_seq, seq[0])

            dve.memset(eps_c[:], EPS)
            dve.memset(ones[:], 1.0)
            dve.memset(ones3[:], 1.0)
            dve.memset(carry[:], 0.0)
            dve.memset(o_sb[:], 0.0)
            dve.memset(bank[:, 7, 0:E * LPE], 0.0)
            dve.memset(zeros, 0.0).then_inc(setup_dve, 1)
            def stats(par):
                for j in range(G):
                    ins = dve.bn_stats(bstat[:, j, :], xt_in[:, par, j, :])
                return ins

            def aggr(par):
                for j in range(G):
                    ins = dve.bn_aggr(mv[:, par, j, :], bstat[:, j, :])
                return ins

            dve.wait_ge(x_in[0], 16)
            stats(0).then_inc(stats_done, 1)
            dve.wait_ge(stats_done, 1)
            aggr(0).then_inc(aggr_done, 1)
            with dve.Fori(0, NGRP // 2) as ii:
                for par in range(2):
                    dve.wait_ge(x_in[1 - par], 16 * (ii + 1 + par))
                    dve.wait_ge(aggr_done, ii * 2 + par + 1)
                    stats(1 - par).then_inc(stats_done, 1)
                    dve.wait_ge(stats_done, ii * 2 + par + 2)
                    settle(dve)
                    dve.wait_ge(xn_done, ii * 2 + par + 1)
                    settle(dve)
                    aggr(1 - par).then_inc(aggr_done, 1)
                    dve.wait_ge(std_done, ii * 2 + par + 1)
                    dve.reciprocal(rstd[:, par, :], rstd[:, par, :]).then_inc(rstd_done, 1)
                    dve.wait_ge(rstd_done, ii * 2 + par + 1)
                    dve.wait_ge(xn_out[par], 16 * ii + 1)
                    dve.wait_ge(turned, ii * 2 + 1)
                    dve.wait_ge(skip_done, ii * 2 + 1)
                    for j in range(G):
                        ins = dve.tensor_scalar(xn[:, par, j, :], xt_in[:, par, j, :], mv[:, par, j, 0:1],
                                                rstd[:, par, j:j + 1], ALU.subtract, ALU.mult)
                    ins.then_inc(xn_done, 1)

            dve.wait_ge(logits_done, NGRP + 1)
            dve.wait_ge(consts_in, 16 * 8)
            link(dve.tensor_copy(logit.rearrange("p i e -> p (i e)"), bank[:, 4:6, :].rearrange("p b c -> p (b c)")))
            per_e = lambda t: t.unsqueeze(1).to_broadcast([P, NT, E])
            per_i = lambda t: t.unsqueeze(2).to_broadcast([P, NT, E])
            for k in range(2):
                link(dve.tensor_reduce(mx[k][:], logit, AX, ALU.max))
                link(dve.tensor_tensor(pos, logit, per_i(mx[k][:]), ALU.is_equal))
                link(dve.tensor_tensor(pos, pos, per_e(emin[:]), ALU.mult))
                link(dve.tensor_reduce(idx[k][:], pos, AX, ALU.min))
                link(dve.tensor_tensor(oh[k], per_e(emin[:]), per_i(idx[k][:]), ALU.is_equal))
                if k == 0:
                    link(dve.scalar_tensor_tensor(out=logit, in0=oh[0], scalar=-3.0e38, in1=logit,
                                                  op0=ALU.mult, op1=ALU.add))
            dve.tensor_tensor(wk[1][:], mx[1][:], mx[0][:], ALU.subtract).then_inc(gate_in, 3)

            tot = bank[:, 2:4, :].rearrange("p b c -> p (b c)").rearrange("p (i e) -> p i e", e=E)
            before = bank[:, 0:2, :].rearrange("p b c -> p (b c)").rearrange("p (i e) -> p i e", e=E)
            for k in range(2):
                dve.wait_ge(pe_route, k + 1)
                for ee in range(E):
                    init = 0.0 if k == 0 else map_g[:, ee:ee + 1]
                    ins = dve.tensor_tensor_scan(pos[:, :, ee], ones[:, 0:NT], tot[:, :, ee], init, ALU.mult, ALU.add)
                link(ins)
                if k == 0:
                    dve.tensor_copy(map_g[:, 0:E], pos[:, NT - 1, :])
                link(dve.tensor_tensor(logit, pos, tot, ALU.subtract))
                link(dve.tensor_tensor(logit, logit, before, ALU.add))
                link(dve.tensor_tensor(logit, logit, oh[k], ALU.mult))
                link(dve.tensor_reduce(loc[k][:], logit, AX, ALU.add))
                dve.sem_inc(gate_out, 1)
                link(dve.tensor_copy(tmp_i[:], loc[k][:]))
                link(dve.tensor_scalar(tmp_i2[:], tmp_i[:], LPE - 1, None, ALU.bitwise_and))
                link(dve.tensor_copy(col[:, k, :], tmp_i2[:]))
                link(dve.tensor_tensor(prt[:, k, :], loc[k][:], col[:, k, :], ALU.subtract))
                link(dve.tensor_scalar(prt[:, k, :], prt[:, k, :], 1.0 / LPE, None, ALU.mult))
                link(dve.tensor_scalar(idx[k][:], idx[k][:], float(E), float(LPE), ALU.add, ALU.mult))
                link(dve.tensor_tensor(col[:, k, :], col[:, k, :], idx[k][:], ALU.add))
                link(dve.tensor_scalar(loc[k][:], loc[k][:], float(CAP), None, ALU.is_lt))
                link(dve.tensor_scalar(idx[k][:], loc[k][:], -BIG, BIG, ALU.mult, ALU.add))
                link(dve.tensor_tensor(col[:, k, :], col[:, k, :], idx[k][:], ALU.add))
            dve.wait_ge(setup_act, 3)
            link(dve.tensor_scalar(mx[0][:], wk[1][:], 1.0, None, ALU.add))
            link(dve.reciprocal(mx[1][:], mx[0][:]))
            link(dve.tensor_tensor(wk[0][:], mx[1][:], loc[0][:], ALU.mult))
            link(dve.tensor_tensor(mx[0][:], mx[1][:], wk[1][:], ALU.mult))
            link(dve.tensor_tensor(wk[1][:], mx[0][:], loc[1][:], ALU.mult))
            prt_f = prt[:].rearrange("p k i -> p (k i)")
            col_f = col[:].rearrange("p k i -> p (k i)")
            dve.sem_inc(oh_used, 4)
            with dve.Fori(0, 2 * NT // 4) as i:
                for r in range(4):
                    dve.wait_ge(oh_used, i * 4 + r + 1)
                    dve.tensor_scalar(oh_p[:, r, :], iota[:, 0:P], prt_f[:, bass.ds(i * 4 + r, 1)], None, ALU.is_equal)
                    dve.tensor_scalar(oh_c[:, r, :], iota[:], col_f[:, bass.ds(i * 4 + r, 1)],
                                      tokval[:, bass.ds(i * 4 + r, 1)], ALU.is_equal, ALU.mult).then_inc(oh_ready, 1)
            link(dve.tensor_copy(b2_q, b2_f))
            link(dve.tensor_tensor(b2_r, b2_f, b2_q, ALU.subtract))
            link(dve.tensor_scalar(b2_p[:], b2_q, ident[0:3, 0:1], None, ALU.mult))
            link(dve.tensor_copy(b2_q, b2_r))
            link(dve.tensor_tensor(b2_r, b2_r, b2_q, ALU.subtract))
            link(dve.scalar_tensor_tensor(out=b2_p[:], in0=b2_q, scalar=ident[0:3, 1:2], in1=b2_p[:],
                                          op0=ALU.mult, op1=ALU.add))
            link(dve.tensor_copy(b2_q, b2_r))
            link(dve.scalar_tensor_tensor(out=b2_p[:], in0=b2_q, scalar=ident[0:3, 2:3], in1=b2_p[:],
                                          op0=ALU.mult, op1=ALU.add))
            dve.wait_ge(oh_used, 2 * NT + 4)
            link(dve.tensor_scalar(map_f[:], bank[:, 7, 0:E * LPE], -1.0, None, ALU.add))
            link(dve.tensor_scalar(map_g[:], map_f[:], 0.0, 2.0 * T + 1.0, ALU.is_lt, ALU.mult))
            link(dve.memset(slot_dst[:], 2 * T + 1))
            link(dve.tensor_tensor(slot_dst[:, SJ:SJ + E * LPE], map_f[:], map_g[:], ALU.add))
            dve.tensor_scalar(slot_tok[:], slot_dst[:], T - 1, None, ALU.bitwise_and).then_inc(map_ready, 1)

            dve.sem_inc(scan_done, SCAN0)
            with dve.Fori(0, E) as e:
                with dve.Fori(0, HPE) as hh:
                    with dve.Fori(0, N // NG) as ng:
                        st = (e * HPE + hh) * (N // NG) + ng
                        dve.wait_ge(carry_done, st + 1)
                        for k in range(NG):
                            for dh in range(KD):
                                p = 2 * k + dh
                                dve.wait_ge(a_ready, st * 2 * NG + p + 2)
                                dve.wait_ge(u_ready, st * 2 * NG + p + 2)
                                dve.tensor_tensor_scan(
                                    h[:, p, :], a_ps[dh], u[:, p % 4, :],
                                    carry[:, bass.ds(hh % 2, 1), bass.ds(dh * N + ng * NG + k, 1)]
                                    .rearrange("p a n -> p (a n)"), ALU.mult, ALU.add).then_inc(scan_done, 1)
                            dve.wait_ge(c_ready, st * NG + k + 2)
                            dve.wait_ge(nsum_done, st * NG + k - 1 + NSUM0)
                            for dh in range(KD):
                                p = 2 * k + dh
                                dve.wait_ge(scan_done, st * 2 * NG + p + 1 + SCAN0)
                                dve.tensor_tensor(hc[:, p % 4, :], h[:, p, :], c_ps, ALU.mult).then_inc(hc_done, 1)
                        dve.wait_ge(hc_done, (st + 1) * 2 * NG + 1)
                        dve.tensor_copy(carry[:, 1, :].rearrange("p (k n) -> p n k", k=KD)[:, bass.ds(ng * NG, NG), :],
                                        h[:, :, HALF - 1].rearrange("p (n k) -> p n k", k=KD)).then_inc(carry_done, 1)

            with dve.Fori(0, NGRP // 2) as ii:
                for par in range(2):
                    dve.wait_ge(fin_in[par], 48 * (ii + 1))
                    dve.wait_ge(fin_done, (ii * 2 + par) * G + 1)
                    for j in range(G):
                        ins = dve.scalar_tensor_tensor(out=xn[:, par, j, :], in0=xt_in[:, par, j, :],
                                                       scalar=wk[0][:, bass.ds((ii * 2 + par) * G + j, 1)],
                                                       in1=xn[:, par, j, :], op0=ALU.mult, op1=ALU.add)
                    ins.then_inc(fin_mid, 1)
                    dve.wait_ge(fin_mid, ii * 2 + par + 1)
                    dve.wait_ge(fin_out[par], 16 * ii + 1)
                    o = xnt_out[:, par].rearrange("p k (j d) -> p (k j) d", d=D)
                    for j in range(G):
                        dve.scalar_tensor_tensor(out=o[:, j, :], in0=xbase[:, par, j, :],
                                                 scalar=wk[1][:, bass.ds((ii * 2 + par) * G + j, 1)],
                                                 in1=xn[:, par, j, :], op0=ALU.mult, op1=ALU.add).then_inc(fin_done, 1)


def kernel(**inputs):
    import numpy as np
    import ml_dtypes
    import concourse.bacc as bacc
    from concourse.bass_utils import run_bass_kernel_spmd

    g = {n: np.asarray(a) for n, a in inputs.items()}
    x = g["L0_attn_x"]
    D = x.shape[2]
    N = g["L0_attn_log_A"].shape[1]
    E, H = g["L0_ffn_b1"].shape
    T = x.shape[0] * x.shape[1]
    lpe = 2 * T // E // P
    sel = np.zeros((96, N, P), ml_dtypes.bfloat16)
    for n in range(N):
        for part in range(3):
            sel[part * 32 + n, n, :] = 1
    arrays = {
        "x": x,
        "log_a": np.concatenate([g["L0_attn_log_A"][:P], g["L0_attn_log_A"][P:]], axis=1),
        "bc_wt": np.concatenate([g["L0_attn_C_w"]] * 3 + [g["L0_attn_B_w"]], axis=0).T,
        "bc_b": np.concatenate([g["L0_attn_C_b"]] * 3 + [g["L0_attn_B_b"]])[:, None],
        "d_skip": g["L0_attn_D_skip"],
        "dt_wt": g["L0_attn_dt_w"].T,
        "dt_b": g["L0_attn_dt_b"].reshape(D // P, P).T,
        "wg": g["L0_ffn_wg"],
        "w1": g["L0_ffn_w1"],
        "b1_t": g["L0_ffn_b1"].reshape(E * H // P, P).T,
        "w2": g["L0_ffn_w2"],
        "b2": g["L0_ffn_b2"].reshape(-1),
        "ident_d": np.eye(P, dtype=np.float32),
        "upper_d": np.triu(np.ones((P, P), np.float32), 1),
        "emin_d": np.tile(np.arange(E, dtype=np.float32) - E, (P, 1)),
        "iota_d": np.tile(np.arange(E * lpe, dtype=np.float32), (P, 1)),
        "tokval_d": (1 + np.arange(2 * T // P, dtype=np.float32)[None, :] * P
                     + np.arange(P, dtype=np.float32)[:, None]),
        "sel_d": sel.reshape(96, N * P),
    }
    arrays = {n: np.ascontiguousarray(a) for n, a in arrays.items()}
    nc = bacc.Bacc("TRN2", target_bir_lowering=False, num_devices=1)
    args = [nc.dram_tensor(n, a.shape, mybir.dt.from_np(a.dtype), kind="ExternalInput").ap() for n, a in arrays.items()]
    out = nc.dram_tensor("out_rows", x.shape, F32, kind="ExternalOutput").ap()
    ssm_moe(nc, *args, out)
    r = run_bass_kernel_spmd(nc, [arrays], core_ids=[0])
    return r.results[0]["out_rows"]
```

```python
from contextlib import ExitStack

import concourse.bass as bass
from concourse import mybir

ALU = mybir.AluOpType
ACT = mybir.ActivationFunctionType
AX = mybir.AxisListType.X
F32 = mybir.dt.float32
BF16 = mybir.dt.bfloat16
I32 = mybir.dt.int32

P = 128
EPS = 1e-5


def ssm_moe(nc, x, log_a, bc_wt, bc_b, d_skip, dt_wt, dt_b, wg, w1, b1_t, w2, b2,
            ident_d, upper_d, emin_d, iota_d, tokval_d, sel_d, out):
    B, S, D = x.shape
    T = B * S
    N = log_a.shape[1] // 2
    E, _, H = w1.shape
    CAP = 2 * T // E
    NT = T // P
    KD = D // P
    HALF = S // 2
    TB = HALF // P
    NG = 8
    STEPS = B * 2 * (N // NG)
    SPE = STEPS // E
    HPE = SPE // (N // NG)
    G = 4
    U = 4
    NGRP = NT // G
    HC = H // P
    SL = 2 * T // STEPS
    SJ = SL // P
    Q = S // NG
    LPE = CAP // P
    BIG = float(1 << 20)

    xf = x.rearrange("b s d -> (b s) d")
    outf = out.rearrange("b s d -> (b s) d")
    xn_d = nc.dram_tensor("xn_rows", [T, D + 2], F32, kind="Internal").ap()
    xnt_d = nc.dram_tensor("xn_transposed", [KD, P, T], F32, kind="Internal").ap()
    b_d = nc.dram_tensor("b_rows", [2 * N, S], F32, kind="Internal").ap()

    def groups(a):
        return a.rearrange("(i j p) d -> i p j d", p=P, j=G)

    with ExitStack() as ctx:
        def sb(name, shape, dt=F32):
            return ctx.enter_context(nc.sbuf_tensor(name, shape, dt))

        def sem(name):
            return ctx.enter_context(nc.semaphore(name))

        bank = ctx.enter_context(nc.psum_tensor("bank", [P, 8, 512], F32))

        ident = sb("ident", [P, P])
        upper = sb("upper", [P, P])
        ones = sb("ones", [P, P])
        emin = sb("emin", [P, E])
        iota = sb("iota", [P, E * LPE])
        tokval = sb("tokval", [P, 2 * NT])
        sel = sb("sel", [96, N * P], BF16)
        ones3 = sb("ones3", [3, P], BF16)
        zeros3 = sb("zeros3", [3, 512], BF16)
        dskip = sb("dskip", [P, D])
        wg_sb = sb("wg_sb", [P, KD, E])
        a_neg = sb("a_neg", [P, KD * N])
        dtw = sb("dtw", [P, KD, D])
        dtb = sb("dtb", [P, KD])
        bcw = sb("bcw", [P, KD, P])
        bcb = sb("bcb", [P, 1])
        b1_sb = sb("b1_sb", [P, E * HC])
        b2_p = sb("b2_p", [3, E * D], BF16)
        w1_sb = sb("w1_sb", [P, KD, H])
        w2_sb = sb("w2_sb", [P, HC, D])
        h = sb("h", [P, 2 * NG, HALF])
        h_flat = h[:].rearrange("p a t -> p (a t)")
        xt_in, xn = (h_flat[:, i * U * G * D:(i + 1) * U * G * D].rearrange("p (a j d) -> p a j d", a=U, d=D)
                     for i in range(2))
        bstat = sb("bstat", [P, G, 6])
        mv = sb("mv", [P, 2, G, 2])
        rstd = sb("rstd", [P, 2, G])
        eps_c = sb("eps_c", [P, 1])
        b_sb = sb("b_sb", [P, 2, NG, HALF])
        logit, pos, oh0, oh1 = (b_sb[:, 1, 2 * i:2 * i + 2, :].rearrange("p a t -> p (a t)")
                                .rearrange("p (i e) -> p i e", e=E) for i in range(4))
        oh = [oh0, oh1]
        hc = sb("hc", [P, 4, HALF])
        small = iter(hc[:].rearrange("p a (b i) -> p (a b) i", i=NT)[:, n, :] for n in range(4 * HALF // NT))
        mx, idx, loc = ([next(small) for _ in range(2)] for _ in range(3))
        prt, col = (hc[:].rearrange("p a t -> p (a t)")[:, n * NT:(n + 2) * NT] for n in (6, 8))
        prt, col = (t.rearrange("p (k i) -> p k i", k=2) for t in (prt, col))
        e2 = hc[:, 3, HALF - NT:]
        tmp_i, tmp_i2 = (hc[:, 3, n * NT:(n + 1) * NT].bitcast(I32) for n in range(2))
        gates = sb("gates", [P, NT, 2])
        u = sb("u", [P, 4, HALF])
        u_flat = u[:].rearrange("p a t -> p (a t)")
        oh_p = u_flat[:, 0:4 * P].rearrange("p (r c) -> p r c", r=4)
        oh_c = u_flat[:, 4 * P:4 * P + 4 * E * LPE].rearrange("p (r c) -> p r c", r=4)
        map_f = sb("map_f", [P, E * LPE])
        map_g = sb("map_g", [P, E * LPE])
        slot_dst = sb("slot_dst", [P, SJ + E * LPE + SJ], I32)
        slot_tok = sb("slot_tok", [P, SJ + E * LPE + SJ], I32)
        slot_k = sb("slot_k", [P, E * LPE, 2])
        xnt = sb("xnt", [P, 2, KD, S])
        dt = sb("dt", [P, 2, KD, S])
        dtx = sb("dtx", [P, 2, KD, S])
        xbase = dt[:, 0].rearrange("p k t -> p (k t)").rearrange("p (a j d) -> p a j d", a=2, d=D)
        xnt_out = dtx[:, 0].rearrange("p k t -> p (k t)").rearrange("p (a k t) -> p a k t", a=2, k=KD)
        c_p = sb("c_p", [96, 2, S], BF16)
        carry = sb("carry", [P, 2, KD * N])
        y_sb = sb("y_sb", [P, 2, TB, D])
        b2_f = dt[0:3, 1].rearrange("p k t -> p (k t)")
        b2_r = dtx[0:3, 1].rearrange("p k t -> p (k t)")
        b2_q = y_sb[0:3, 0].rearrange("p j d -> p (j d)").bitcast(BF16)
        za = sb("za", [P, KD, Q])
        zr = sb("zr", [P, KD, Q])
        ze = sb("ze", [P, KD, Q])
        zl = sb("zl", [P, KD, Q])
        bcv = sb("bcv", [P, Q])
        c_r = sb("c_r", [96, Q])
        gidx = sb("gidx", [P, SJ], I32)
        sidx = sb("sidx", [P, SJ], I32)
        xg = sb("xg", [P, SJ, D + 2])
        gate2 = sb("gate2", [P, SJ, 2])
        gate = sb("gate", [P, SJ])
        xgt = sb("xgt", [P, KD, SL])
        ht = sb("ht", [P, HC, SL])
        o_sb = sb("o_sb", [P, SJ, D])

        y_ps = bank[:, 0:2, :]
        y_blk = y_ps.rearrange("p b (t d) -> p (b t) d", d=D)
        a_ps = [bank[:, 2, :], bank[:, 3, :]]
        c_ps = bank[:, 4, :]
        m_ps = [bank[:, 5, :], bank[:, 6, :]]

        waits_passed = sem("waits_passed")
        consts_in = sem("consts_in")
        weights_in = sem("weights_in")
        x_in = [sem(f"x_in{i}") for i in range(U)]
        stats_done = sem("stats_done")
        aggr_done = sem("aggr_done")
        std_done = sem("std_done")
        rstd_done = sem("rstd_done")
        xn_done = sem("xn_done")
        xn_out = [sem(f"xn_out{i}") for i in range(U)]
        xnt_st = [sem(f"xnt_st{i}") for i in range(2)]
        base_out = [sem(f"base_out{i}") for i in range(2)]
        skip_done = sem("skip_done")
        base_done = sem("base_done")
        turned = sem("turned")
        xnt_done = sem("xnt_done")
        logits_done = sem("logits_done")
        dve_seq = sem("dve_seq")
        pe_route = sem("pe_route")
        gate_in = sem("gate_in")
        gate_out = sem("gate_out")
        oh_ready = sem("oh_ready")
        oh_used = sem("oh_used")
        map_ready = sem("map_ready")
        gates_ready = sem("gates_ready")
        gates_out = sem("gates_out")
        setup_act = sem("setup_act")
        setup_dve = sem("setup_dve")
        xnt_in = sem("xnt_in")
        b_in = sem("b_in")
        b_st = sem("b_st")
        w1_in = sem("w1_in")
        w2_in = sem("w2_in")
        xg_in = sem("xg_in")
        gidx_done = sem("gidx_done")
        sidx_done = sem("sidx_done")
        o_scattered = sem("o_scattered")
        fill_done = sem("fill_done")
        evac_done = sem("evac_done")
        c_ready = sem("c_ready")
        a_ready = sem("a_ready")
        u_ready = sem("u_ready")
        scan_done = sem("scan_done")
        hc_done = sem("hc_done")
        nsum_done = sem("nsum_done")
        carry_done = sem("carry_done")
        gate_mul = sem("gate_mul")
        gate_ready = sem("gate_ready")
        y_evac = sem("y_evac")
        y_out = sem("y_out")
        z_done = sem("z_done")
        v_done = sem("v_done")
        l_done = sem("l_done")
        dt_done = sem("dt_done")
        r1_done = sem("r1_done")
        r2_done = sem("r2_done")
        c2_done = sem("c2_done")
        c_parts = sem("c_parts")
        prep_done = sem("prep_done")
        FP = NG
        FS = 2 + HC // 2 + SJ
        SCAN0, NSUM0 = 4, 2
        TURNED0, SKIP0, XNT0, LOGITS0 = U, U, 2, 2

        def settle(eng):
            eng.sem_inc(waits_passed, 1)

        def start_at_one(eng, *sems):
            for s in sems:
                eng.sem_inc(s, 1)

        def moe_pieces():
            out = [(0, 0.43, "turn", None), (1, 1.28, "prep", None)]
            for f in range(HC // 2):
                out += [(2 + f, 0.85, "up", (f, c)) for c in range(2)]
            for j in range(SJ):
                out += [(2 + HC // 2 + j, 0.43, "down", (j, hh)) for hh in range(HC)]
                out += [(2 + HC // 2 + j, 0.1, "bias", j)]
            return out

        pieces = moe_pieces()
        total = sum(c for _, c, _, _ in pieces)
        share = [total / (NG - 0.55)] * (NG - 1) + [total]
        slices, at, acc = [], 0, 0.0
        for k in range(NG):
            acc += share[k]
            take = []
            while at < len(pieces) and sum(c for _, c, _, _ in pieces[:at + 1]) <= acc + 0.25:
                take.append(pieces[at])
                at += 1
            slices.append(take)
        slices[-1] += pieces[at:]
        last_of = {}
        for k, take in enumerate(slices):
            for piece in take:
                last_of[piece[0]] = k
        evac_at = {f: min(last_of[f] + 1, NG - 1) for f in last_of}

        block = ctx.enter_context(nc.Block())

        @block.sync
        def _(sp):
            start_at_one(sp, *xn_out, *base_out, b_st)
            for dst, src in ((ident, ident_d), (upper, upper_d), (emin, emin_d), (iota, iota_d),
                             (tokval, tokval_d), (sel, sel_d), (dskip, d_skip.partition_broadcast(P)),
                             (wg_sb, wg.rearrange("(k p) e -> p k e", p=P))):
                sp.dma_start(dst[:], src).then_inc(consts_in, 16)
            x_g, xn_g, out_g = groups(xf), groups(xn_d[:, 0:D]), groups(outf)

            def load_x(par, grp):
                sp.dma_start(xt_in[:, par], x_g[bass.ds(grp, 1)].rearrange("a p j d -> (a p) j d")).then_inc(x_in[par], 16)

            for r in range(U):
                load_x(r, r)
            for dst, src in ((a_neg, log_a), (dtw, dt_wt.rearrange("(k p) e -> p k e", p=P)), (dtb, dt_b),
                             (bcw, bc_wt.rearrange("(k p) e -> p k e", p=P)), (bcb, bc_b),
                             (b1_sb, b1_t), (b2_f, b2.partition_broadcast(3))):
                sp.dma_start(dst if dst is b2_f else dst[:], src).then_inc(weights_in, 16)

            with sp.Fori(0, NGRP // U) as ii:
                for r in range(U):
                    grp = ii * U + r
                    sp.wait_ge(xn_done, grp + 2)
                    sp.dma_start(xn_g[bass.ds(grp, 1)].rearrange("a p j d -> (a p) j d"),
                                 xn[:, r]).then_inc(xn_out[r], 16)
                    sp.wait_ge(base_done, grp + 1)
                    sp.dma_start(out_g[bass.ds(grp, 1)].rearrange("a p j d -> (a p) j d"),
                                 xbase[:, r % 2]).then_inc(base_out[r % 2], 16)
                    sp.wait_ge(stats_done, grp + 1)
                    load_x(r, (grp + U) % NGRP)
            for r in range(2):
                sp.wait_ge(xnt_st[r], 16 * (NGRP // 2) + 1)
                sp.wait_ge(base_out[r], 16 * (NGRP // 2) + 1)
            for r in range(U):
                sp.wait_ge(xn_out[r], 16 * (NGRP // U) + 1)
                sp.wait_ge(x_in[r], 16 * (NGRP // U + 1))

            def load_xnt(par, b):
                src = xnt_d.rearrange("k p t -> p k t")[:, :, bass.ds(b * S, S)]
                sp.dma_start(xnt[:, par], src).then_inc(xnt_in, 16)

            def load_w1(e):
                src = w1[bass.ds(e, 1)].rearrange("a (k p) h -> p (a k) h", p=P)
                sp.dma_start(w1_sb[:], src).then_inc(w1_in, 16)

            def load_w2(e):
                src = w2[bass.ds(e, 1)].rearrange("a (c p) d -> p (a c) d", p=P)
                sp.dma_start(w2_sb[:], src).then_inc(w2_in, 16)

            def load_b(buf, par, th, ng):
                src = b_d[bass.ds(par * N + ng * NG, NG), bass.ds(th * HALF, HALF)].partition_broadcast(P)
                dst = b_sb[:, bass.ds(buf, 1)].rearrange("p a n t -> p (a n) t")
                sp.dma_start(dst, src).then_inc(b_in, 16)

            load_xnt(0, 0)
            sp.wait_ge(xnt_in, 16)
            load_xnt(1, 1)
            load_w1(0)
            load_w2(0)
            with sp.Fori(0, NG) as q:
                sp.wait_ge(evac_done, q + 2)
                sp.dma_start(b_d[0:N, bass.ds(q * Q, Q)], bcv[96:P, :]).then_inc(b_st, 16)
            sp.wait_ge(gates_ready, 1)
            sp.dma_start(xn_d[:, D:D + 2].rearrange("(i p) d -> p i d", p=P), gates[:]).then_inc(gates_out, 16)
            sp.wait_ge(b_st, 16 * NG + 1)
            sp.wait_ge(prep_done, NG + 1)
            sp.wait_ge(xnt_in, 32)
            load_xnt(0, 2)
            load_b(0, 0, 0, 0)
            sp.wait_ge(map_ready, 1)

            with sp.Fori(0, E) as e:
                with sp.Fori(0, HPE) as hh:
                    with sp.Fori(0, N // NG) as ng:
                        st = e * SPE + hh * (N // NG) + ng
                        nx = st + 1
                        sp.wait_ge(u_ready, st * 2 * NG + 1)
                        sp.wait_ge(b_in, 16 * (st + 1))
                        sp.wait_ge(b_st, 16 * (NG + st) + 1)
                        load_b(nx % 2, (nx // NG) % 2, (nx // (N // NG)) % 2, nx % (N // NG))
                        sp.wait_ge(evac_done, FP + st * FS + 2 + 1)
                        settle(sp)
                        sp.dma_start(b_d[bass.ds((1 - hh // 2) * N, N), bass.ds(((hh % 2) * (N // NG) + ng) * Q, Q)],
                                     bcv[96:P, :]).then_inc(b_st, 16)
                    hf = e * HPE + hh
                    sp.wait_ge(prep_done, FP + (hf + 1) * (N // NG) + 1)
                    sp.wait_ge(xnt_in, 16 * (hf + 3))
                    settle(sp)
                    src = xnt_d.rearrange("k p t -> p k t")[:, :, bass.ds((hf // 2 + 3) % B * S + hh % 2 * HALF, HALF)]
                    sp.dma_start(xnt[:, bass.ds(1 - hh // 2, 1), :, bass.ds(hh % 2 * HALF, HALF)]
                                 .rearrange("p a k t -> p (a k) t"), src).then_inc(xnt_in, 16)
                last = FP + (e + 1) * SPE * FS
                sp.wait_ge(fill_done, last - SJ)
                load_w1((e + 1) % E)
                sp.wait_ge(fill_done, last)
                load_w2((e + 1) % E)
            sp.wait_ge(w1_in, 16 * (E + 1))
            sp.wait_ge(w2_in, 16 * (E + 1))
            sp.wait_ge(b_in, 16 * (STEPS + 1))
            sp.wait_ge(b_st, 16 * (NG + STEPS) + 1)
            sp.wait_ge(xnt_in, 16 * (2 * B + 3))

            sp.wait_ge(gates_out, 16)

        @block.tensor
        def _(pe):
            def turn(dst, src, start):
                return pe.matmul(dst, src, ident[:], start=start, stop=True, is_transpose=True, skip_group_check=True)

            start_at_one(pe, c_ready)
            pe.sem_inc(turned, TURNED0)
            pe.sem_inc(logits_done, LOGITS0)
            pe.wait_ge(consts_in, 16 * 8)
            lg_ps = bank[:, 4:6, :].rearrange("p b c -> p (b c)")

            def turn_group(grp, r):
                pe.wait_ge(xn_done, grp + 2)
                pe.wait_ge(xnt_done, grp - 1 + XNT0)
                for k in range(KD):
                    for j in range(G):
                        mm = turn(bank[:, 2 * (r % 2) + k, j * P:(j + 1) * P], xn[:, r % U, j, k * P:(k + 1) * P], True)
                mm.then_inc(turned, 1)

            def logits_group(grp, r):
                pe.wait_ge(xnt_done, grp + 1 + XNT0)
                for j in range(G):
                    for k in range(KD):
                        mm = pe.matmul(lg_ps[:, bass.ds((grp * G + j) * E, E)],
                                       xnt_out[:, r % 2, k, j * P:(j + 1) * P], wg_sb[:, k, :],
                                       start=(k == 0), stop=(k == KD - 1))
                mm.then_inc(logits_done, 1)

            turn_group(0, 0)
            with pe.Fori(0, NGRP // U - 1) as ii:
                for r in range(U):
                    turn_group(ii * U + r + 1, r + 1)
                    logits_group(ii * U + r, r)
            for r in range(U):
                if r < U - 1:
                    turn_group(NGRP - U + r + 1, r + 1)
                logits_group(NGRP - U + r, r)

            def prep(par, q, f):
                for g in range(3):
                    w = dtw[:, :, g * P:(g + 1) * P] if g < 2 else bcw[:]
                    for k in range(KD):
                        src = xnt[:, bass.ds(par, 1), k, bass.ds(q * Q, Q)].rearrange("p a t -> p (a t)")
                        mm = pe.matmul(m_ps[f][:, g * Q:(g + 1) * Q], w[:, k, :], src, start=(k == 0), stop=(k == KD - 1))
                return mm

            def count(k):
                pe.wait_ge(gate_in, k + 1)
                ohf = oh[k].rearrange("p i e -> p (i e)")
                for c in range(2):
                    pe.matmul(bank[:, c, :], upper[:], ohf[:, c * 512:(c + 1) * 512], start=True, stop=True)
                    mm = pe.matmul(bank[:, 2 + c, :], ones[:], ohf[:, c * 512:(c + 1) * 512], start=True, stop=True)
                mm.then_inc(pe_route, 1)

            count(0)
            pe.wait_ge(weights_in, 16 * 7)
            pe.wait_ge(xnt_in, 16)
            with pe.Fori(0, NG // 2) as i:
                for f in range(2):
                    pe.wait_ge(evac_done, i * 2 + f + 1)
                    prep(0, i * 2 + f, f).then_inc(fill_done, 1)
            pe.sem_inc(nsum_done, NSUM0)
            pe.wait_ge(gate_out, 1)
            count(1)
            pe.wait_ge(setup_dve, 1)
            with pe.Fori(0, 2 * NT // 4) as i:
                for r in range(4):
                    pe.wait_ge(oh_ready, i * 4 + r + 1)
                    pe.matmul(bank[:, 7, 0:E * LPE], oh_p[:, r, :], oh_c[:, r, :], start=False, stop=True,
                              skip_group_check=True).then_inc(oh_used, 1)

            with pe.Fori(0, E) as e:
                with pe.Fori(0, HPE) as hh:
                    hf = e * HPE + hh
                    pe.wait_ge(y_evac, hf + 1)
                    for c in range(2):
                        pe.matmul(y_ps[:, c, :], ones3[:], zeros3[:], start=True, stop=True, skip_group_check=True)
                    pe.wait_ge(c_parts, (hf + 1) * (N // NG) + 1)
                    settle(pe)
                    with pe.Fori(0, N // NG) as ng:
                        st = hf * (N // NG) + ng
                        for k in range(NG):
                            pe.wait_ge(hc_done, st * 2 * NG + 2 * k + 1)
                            pe.matmul(c_ps, sel[:, bass.ds(ng * NG * P + k * P, P)],
                                      c_p[:, bass.ds(hh // 2, 1), bass.ds((hh % 2) * HALF, HALF)]
                                      .rearrange("p a t -> p (a t)"), start=True, stop=True).then_inc(c_ready, 1)
                            for n, (f, _, kind, arg) in enumerate(slices[k]):
                                starts = pieces.index(slices[k][n]) == [p[0] for p in pieces].index(f)
                                ends = pieces.index(slices[k][n]) == max(i for i, p in enumerate(pieces) if p[0] == f)
                                m = m_ps[f % 2]
                                if starts:
                                    pe.wait_ge(evac_done, FP + st * FS + f - 1 + 1)
                                if kind == "turn":
                                    pe.wait_ge(xg_in, 16 * SJ * (st + 1))
                                    for kk in range(KD):
                                        for j in range(SJ):
                                            mm = turn(m[:, kk * SL + j * P:kk * SL + (j + 1) * P],
                                                      xg[:, j, kk * P:(kk + 1) * P], True)
                                elif kind == "prep":
                                    pe.wait_ge(xnt_in, 16 * (hf // 2 * 2 + 2))
                                    settle(pe)
                                    mm = prep(1 - hh // 2, (hh % 2) * (N // NG) + ng, f % 2)
                                elif kind == "up":
                                    if arg == (0, 0):
                                        pe.wait_ge(w1_in, 16 * (e + 1))
                                        pe.wait_ge(evac_done, FP + st * FS + 2)
                                    ch = 2 * arg[0] + arg[1]
                                    for kk in range(KD):
                                        mm = pe.matmul(m[:, arg[1] * SL:(arg[1] + 1) * SL],
                                                       w1_sb[:, kk, ch * P:(ch + 1) * P], xgt[:, kk, :],
                                                       start=(kk == 0), stop=(kk == KD - 1))
                                elif kind == "down":
                                    j, c = arg
                                    if c == 0:
                                        pe.wait_ge(w2_in, 16 * (e + 1))
                                    if j == 0 and c % 2 == 0:
                                        pe.wait_ge(evac_done, FP + st * FS + 2 + c // 2 + 2)
                                    mm = pe.matmul(m[:, 0:D], ht[:, c, j * P:(j + 1) * P], w2_sb[:, c, :],
                                                   start=(c == 0), stop=False)
                                else:
                                    mm = pe.matmul(m[:, 0:D], ones3[:], b2_p[:, bass.ds(e * D, D)],
                                                   start=False, stop=True)
                                if ends:
                                    mm.then_inc(fill_done, 1)
                            for dh in range(KD):
                                pe.wait_ge(hc_done, st * 2 * NG + 2 * k + dh + 2)
                                for tb in range(TB):
                                    mm = turn(y_blk[:, tb, dh * P:(dh + 1) * P],
                                              hc[:, (2 * k + dh) % 4, tb * P:(tb + 1) * P], False)
                            mm.then_inc(nsum_done, 1)

        @block.scalar
        def _(act):
            start_at_one(act, *xnt_st, evac_done, a_ready, y_evac, c_parts)
            act.sem_inc(xnt_done, XNT0)
            act.wait_ge(setup_dve, 1)
            act.wait_ge(aggr_done, 1)

            def std(par):
                return act.activation(rstd[:, par, :], mv[:, par, :, 1], ACT.Sqrt, bias=eps_c[:, 0:1])

            xnt_g = xnt_d.rearrange("k p (i t) -> i p k t", t=G * P)
            std(0).then_inc(std_done, 1)
            with act.Fori(0, NGRP // U) as ii:
                for r in range(U):
                    grp = ii * U + r
                    act.wait_ge(aggr_done, grp + 2)
                    act.wait_ge(xn_done, grp + 1)
                    std((r + 1) % 2).then_inc(std_done, 1)
                    act.wait_ge(turned, grp + 1 + TURNED0)
                    act.wait_ge(xnt_st[r % 2], 16 * (ii * (U // 2) + r // 2) + 1)
                    act.wait_ge(logits_done, grp - 1 + LOGITS0)
                    act.activation(xnt_out[:, r % 2].rearrange("p k t -> p (k t)"),
                                   bank[:, 2 * (r % 2):2 * (r % 2) + 2, :].rearrange("p b c -> p (b c)"),
                                   ACT.Copy).then_inc(xnt_done, 1)
                    act.wait_ge(xnt_done, grp + 1 + XNT0)
                    act.dma_start(xnt_g[bass.ds(grp, 1)].rearrange("a p k t -> (a p) k t"),
                                  xnt_out[:, r % 2]).then_inc(xnt_st[r % 2], 16)

            act.preload_act_table_set("natural_log_exp_and_others")
            act.wait_ge(weights_in, 16 * 7)
            act.activation(a_neg[:], a_neg[:], ACT.Exp).then_inc(setup_act, 1)
            act.wait_ge(setup_act, 1)
            act.mul(a_neg[:], a_neg[:], -1.0).then_inc(setup_act, 1)
            act.wait_ge(gate_in, 3)
            act.activation(e2, e2, ACT.Exp).then_inc(setup_act, 1)
            act.wait_ge(setup_act, 3)

            def evac_prep(m, pdone, par, q):
                for g in range(KD):
                    act.activation(za[:, g, :], m[:, g * Q:(g + 1) * Q], ACT.Abs, bias=dtb[:, g:g + 1])
                for g in range(KD):
                    ins = act.activation(zr[:, g, :], m[:, g * Q:(g + 1) * Q], ACT.Relu, bias=dtb[:, g:g + 1])
                ins.then_inc(z_done, 1)
                act.wait_ge(b_st, 16 * pdone + 1)
                act.activation(bcv[:], m[:, 2 * Q:3 * Q], ACT.Identity, bias=bcb[:, 0:1]).then_inc(evac_done, 1)
                act.wait_ge(z_done, pdone + 1)
                act.activation(ze[:], za[:], ACT.Exp, scale=-1.0).then_inc(v_done, 1)
                act.wait_ge(v_done, pdone + 1)
                c1 = c_p[:, bass.ds(par, 1), bass.ds(q * Q, Q)].rearrange("p a t -> p (a t)")
                act.activation(c1, bcv[0:96, :], ACT.Copy)
                act.activation(zl[:], ze[:], ACT.Ln, bias=1.0).then_inc(l_done, 1)

            def c_part2(pdone, par, q):
                act.wait_ge(r1_done, pdone + 1)
                settle(act)
                for r in (32, 64):
                    ins = act.activation(c_p[r:r + 32, bass.ds(par, 1), bass.ds(q * Q, Q)].rearrange("p a t -> p (a t)"),
                                         c_r[r:r + 32, :], ACT.Copy)
                ins.then_inc(c2_done, 1)

            def c_part3(pdone, par, q):
                act.wait_ge(r2_done, pdone + 1)
                settle(act)
                act.activation(c_p[64:96, bass.ds(par, 1), bass.ds(q * Q, Q)].rearrange("p a t -> p (a t)"),
                               c_r[64:96, :], ACT.Copy).then_inc(c_parts, 1)

            with act.Fori(0, NG // 2) as i:
                for f in range(2):
                    act.wait_ge(fill_done, i * 2 + f + 1)
                    act.wait_ge(prep_done, i * 2 + f + 1)
                    evac_prep(m_ps[f], i * 2 + f, 0, i * 2 + f)
                    c_part2(i * 2 + f, 0, i * 2 + f)
                    c_part3(i * 2 + f, 0, i * 2 + f)

            with act.Fori(0, E) as e:
                with act.Fori(0, HPE) as hh:
                    hf = e * HPE + hh
                    act.wait_ge(prep_done, (hf + 1) * (N // NG) + 1)
                    with act.Fori(0, N // NG) as ng:
                        st = hf * (N // NG) + ng
                        for k in range(NG):
                            for dh in range(KD):
                                act.wait_ge(scan_done, st * 2 * NG + 2 * k + dh - 1 + SCAN0)
                                act.activation(a_ps[dh],
                                               dt[:, bass.ds(hh // 2, 1), dh, bass.ds((hh % 2) * HALF, HALF)]
                                               .rearrange("p a t -> p (a t)"), ACT.Exp,
                                               scale=a_neg[:, bass.ds(dh * N + ng * NG + k, 1)]).then_inc(a_ready, 1)
                            for f in sorted(evac_at):
                                if evac_at[f] != k:
                                    continue
                                m = m_ps[f % 2]
                                act.wait_ge(fill_done, FP + st * FS + f + 1)
                                if f == 0:
                                    act.activation(xgt[:].rearrange("p k s -> p (k s)"), m,
                                                   ACT.Copy).then_inc(evac_done, 1)
                                elif f == 1:
                                    act.wait_ge(prep_done, FP + st + 1)
                                    evac_prep(m, FP + st, 1 - hh // 2, (hh % 2) * (N // NG) + ng)
                                elif f < 2 + HC // 2:
                                    if f == 2 + HC // 2 - 1:
                                        act.wait_ge(o_scattered, 16 * SJ * (st + 1))
                                    for c in range(2):
                                        ch = 2 * (f - 2) + c
                                        ins = act.activation(ht[:, ch, :], m[:, c * SL:(c + 1) * SL], ACT.Relu,
                                                             bias=b1_sb[:, bass.ds(e * HC + ch, 1)])
                                    ins.then_inc(evac_done, 1)
                                else:
                                    j = f - 2 - HC // 2
                                    if j == 0:
                                        act.wait_ge(gate_ready, st + 1)
                                    act.activation(o_sb[:, j, :], m[:, 0:D], ACT.Copy,
                                                   scale=gate[:, j:j + 1]).then_inc(evac_done, 1)
                            if k == 5:
                                c_part2(FP + st, 1 - hh // 2, (hh % 2) * (N // NG) + ng)
                            if k == 7:
                                c_part3(FP + st, 1 - hh // 2, (hh % 2) * (N // NG) + ng)
                    act.wait_ge(nsum_done, (hf + 1) * N + NSUM0)
                    act.wait_ge(y_out, 16 * (hf + 1))
                    act.activation(y_sb[:, bass.ds(hh % 2, 1)].rearrange("p a j d -> p (a j d)"),
                                   y_ps.rearrange("p b c -> p (b c)"), ACT.Copy).then_inc(y_evac, 1)

        @block.gpsimd
        def _(pool):
            start_at_one(pool, u_ready)
            pool.sem_inc(skip_done, SKIP0)
            pool.wait_ge(consts_in, 16 * 8)
            dsk = dskip[:].unsqueeze(1).to_broadcast([P, G, D])
            with pool.Fori(0, NGRP // U) as ii:
                for r in range(U):
                    grp = ii * U + r
                    pool.wait_ge(xn_done, grp + 2)
                    pool.wait_ge(base_out[r % 2], 16 * (ii * (U // 2) + r // 2) + 1)
                    pool.tensor_tensor(xbase[:, r % 2], xn[:, r], dsk, ALU.mult).then_inc(skip_done, 1)
                    pool.wait_ge(skip_done, grp + 1 + SKIP0)
                    pool.tensor_tensor(xbase[:, r % 2], xbase[:, r % 2], xt_in[:, r], ALU.add).then_inc(base_done, 1)

            def gather(st, nx):
                pool.tensor_copy(gidx[:], slot_tok[:, bass.ds(nx * SJ + SJ, SJ)]).then_inc(gidx_done, 1)
                pool.wait_ge(gidx_done, nx + 1)
                settle(pool)
                for j in range(SJ):
                    pool.indirect_dma_start(xg[:, j, :], None, xn_d, bass.IndirectOffsetOnAxis(ap=gidx[:, j:j + 1], axis=0),
                                            bounds_check=T - 1, oob_is_err=False).then_inc(xg_in, 16)

            def scatter(st):
                pool.tensor_copy(sidx[:], slot_dst[:, bass.ds(st * SJ, SJ)]).then_inc(sidx_done, 1)
                pool.wait_ge(sidx_done, st + 1)
                settle(pool)
                for j in range(SJ):
                    pool.indirect_dma_start(outf, bass.IndirectOffsetOnAxis(ap=sidx[:, j:j + 1], axis=0), o_sb[:, j, :], None,
                                            bounds_check=T - 1, oob_is_err=False, compute_op=ALU.add).then_inc(o_scattered, 16)

            def add_y(hf, buf):
                pool.dma_start(groups(outf)[bass.ds(hf, 1)].rearrange("a p j d -> (a p) j d"),
                               y_sb[:, bass.ds(buf, 1)].rearrange("p a j d -> p (a j) d"), accum_op=ALU.add
                               ).then_inc(y_out, 16)

            pool.wait_ge(map_ready, 1)
            for r in range(U):
                pool.wait_ge(xn_out[r], 16 * (NGRP // U) + 1)
            for r in range(2):
                pool.wait_ge(base_out[r], 16 * (NGRP // 2) + 1)
            pool.wait_ge(gates_out, 16)
            gather(0, 0)

            with pool.Fori(0, E) as e:
                with pool.Fori(0, HPE) as hh:
                    hf = e * HPE + hh
                    pool.wait_ge(evac_done, FP + hf * (N // NG) * FS - SJ + 1)
                    pool.wait_ge(y_evac, hf)
                    settle(pool)
                    add_y((hf + 2 * B - 2) % (2 * B), hh % 2)
                    pool.wait_ge(prep_done, (hf + 1) * (N // NG) + 1)
                    settle(pool)
                    with pool.Fori(0, N // NG) as ng:
                        st = hf * (N // NG) + ng
                        pool.wait_ge(b_in, 16 * (st + 1))
                        for k in range(NG):
                            for dh in range(KD):
                                p = 2 * k + dh
                                pool.wait_ge(scan_done, st * 2 * NG + p - 3 + SCAN0)
                                settle(pool)
                                pool.tensor_tensor(u[:, p % 4, :],
                                                   dtx[:, bass.ds(hh // 2, 1), dh, bass.ds((hh % 2) * HALF, HALF)]
                                                   .rearrange("p a t -> p (a t)"),
                                                   b_sb[:, bass.ds(st % 2, 1), k, :].rearrange("p a t -> p (a t)"),
                                                   ALU.mult).then_inc(u_ready, 1)
                            if k == 2:
                                pool.wait_ge(evac_done, FP + st * FS + 1)
                                pool.wait_ge(y_out, 16 * (hf + 1))
                                scatter(st)
                            if k == 4:
                                pool.wait_ge(fill_done, FP + st * FS + 1)
                                pool.wait_ge(gate_ready, st + 1)
                                gather(st, st + 1)
            pool.wait_ge(evac_done, FP + STEPS * FS + 1)
            scatter(STEPS)
            pool.wait_ge(o_scattered, 16 * SJ * (STEPS + 1))
            for n in range(2):
                pool.wait_ge(y_evac, 2 * B + n)
                add_y(2 * B - 2 + n, n)
                pool.wait_ge(y_out, 16 * (2 * B + 1 + n))
            pool.wait_ge(xg_in, 16 * SJ * (STEPS + 1))

        @block.vector
        def _(dve):
            start_at_one(dve, xn_done, hc_done, carry_done, prep_done)
            seq = [0]

            def link(ins):
                seq[0] += 1
                ins.then_inc(dve_seq, 1)
                dve.wait_ge(dve_seq, seq[0])

            dve.memset(eps_c[:], EPS)
            dve.memset(ones[:], 1.0)
            dve.memset(ones3[:], 1.0)
            dve.memset(carry[:], 0.0)
            dve.memset(o_sb[:], 0.0)
            dve.memset(bank[:, 7, 0:E * LPE], 0.0)
            dve.memset(zeros3[:], 0.0).then_inc(setup_dve, 1)
            def stats(par):
                for j in range(G):
                    ins = dve.bn_stats(bstat[:, j, :], xt_in[:, par, j, :])
                return ins

            def aggr(par):
                for j in range(G):
                    ins = dve.bn_aggr(mv[:, par, j, :], bstat[:, j, :])
                return ins

            dve.wait_ge(x_in[0], 16)
            stats(0).then_inc(stats_done, 1)
            dve.wait_ge(stats_done, 1)
            aggr(0).then_inc(aggr_done, 1)
            with dve.Fori(0, NGRP // U) as ii:
                for r in range(U):
                    grp, s2 = ii * U + r, r % 2
                    dve.wait_ge(x_in[(r + 1) % U], 16 * (ii + 1 + (r + 1) // U))
                    dve.wait_ge(aggr_done, grp + 1)
                    stats((r + 1) % U).then_inc(stats_done, 1)
                    dve.wait_ge(stats_done, grp + 2)
                    settle(dve)
                    dve.wait_ge(xn_done, grp + 1)
                    settle(dve)
                    aggr(1 - s2).then_inc(aggr_done, 1)
                    dve.wait_ge(std_done, grp + 1)
                    dve.reciprocal(rstd[:, s2, :], rstd[:, s2, :]).then_inc(rstd_done, 1)
                    dve.wait_ge(rstd_done, grp + 1)
                    dve.wait_ge(xn_out[r], 16 * ii + 1)
                    dve.wait_ge(turned, grp - U + 1 + TURNED0)
                    dve.wait_ge(skip_done, grp - U + 1 + SKIP0)
                    for j in range(G):
                        ins = dve.tensor_scalar(xn[:, r, j, :], xt_in[:, r, j, :], mv[:, s2, j, 0:1],
                                                rstd[:, s2, j:j + 1], ALU.subtract, ALU.mult)
                    ins.then_inc(xn_done, 1)

            dve.wait_ge(logits_done, NGRP + LOGITS0)
            dve.wait_ge(consts_in, 16 * 8)
            link(dve.tensor_copy(logit.rearrange("p i e -> p (i e)"), bank[:, 4:6, :].rearrange("p b c -> p (b c)")))
            per_e = lambda t: t.unsqueeze(1).to_broadcast([P, NT, E])
            per_i = lambda t: t.unsqueeze(2).to_broadcast([P, NT, E])
            for k in range(2):
                link(dve.tensor_reduce(mx[k], logit, AX, ALU.max))
                link(dve.tensor_tensor(pos, logit, per_i(mx[k]), ALU.is_equal))
                link(dve.tensor_tensor(pos, pos, per_e(emin[:]), ALU.mult))
                link(dve.tensor_reduce(idx[k], pos, AX, ALU.min))
                link(dve.tensor_tensor(oh[k], per_e(emin[:]), per_i(idx[k]), ALU.is_equal))
                if k == 0:
                    link(dve.scalar_tensor_tensor(out=logit, in0=oh[0], scalar=-3.0e38, in1=logit,
                                                  op0=ALU.mult, op1=ALU.add))
                dve.sem_inc(gate_in, 1)
            dve.tensor_tensor(e2, mx[1], mx[0], ALU.subtract).then_inc(gate_in, 1)

            def prep_dt(pdone, par, q):
                dst = lambda t: t[:, bass.ds(par, 1), :, bass.ds(q * Q, Q)].rearrange("p a k t -> p (a k) t")
                dve.wait_ge(l_done, pdone + 1)
                dve.tensor_tensor(dst(dt), zr[:], zl[:], ALU.add).then_inc(dt_done, 1)
                dve.wait_ge(c_parts, pdone + 1)
                c_all = c_p[:, bass.ds(par, 1), bass.ds(q * Q, Q)].rearrange("p a t -> p (a t)")
                dve.tensor_tensor(c_r[:], bcv[0:96, :], c_all, ALU.subtract).then_inc(r1_done, 1)
                dve.wait_ge(dt_done, pdone + 1)
                dve.tensor_tensor(dst(dtx), dst(dt), dst(xnt), ALU.mult).then_inc(prep_done, 1)

            def prep_c(pdone, par, q):
                dve.wait_ge(c2_done, pdone + 1)
                c_all = c_p[:, bass.ds(par, 1), bass.ds(q * Q, Q)].rearrange("p a t -> p (a t)")
                dve.tensor_tensor(c_r[:], c_r[:], c_all, ALU.subtract).then_inc(r2_done, 1)

            with dve.Fori(0, NG) as q:
                prep_dt(q, 0, q)
                prep_c(q, 0, q)

            tot = bank[:, 2:4, :].rearrange("p b c -> p (b c)").rearrange("p (i e) -> p i e", e=E)
            before = bank[:, 0:2, :].rearrange("p b c -> p (b c)").rearrange("p (i e) -> p i e", e=E)
            for k in range(2):
                dve.wait_ge(pe_route, k + 1)
                for ee in range(E):
                    init = 0.0 if k == 0 else map_g[:, ee:ee + 1]
                    ins = dve.tensor_tensor_scan(pos[:, :, ee], ones[:, 0:NT], tot[:, :, ee], init, ALU.mult, ALU.add)
                link(ins)
                if k == 0:
                    dve.tensor_copy(map_g[:, 0:E], pos[:, NT - 1, :])
                link(dve.tensor_tensor(logit, pos, tot, ALU.subtract))
                link(dve.tensor_tensor(logit, logit, before, ALU.add))
                link(dve.tensor_tensor(logit, logit, oh[k], ALU.mult))
                link(dve.tensor_reduce(loc[k], logit, AX, ALU.add))
                dve.sem_inc(gate_out, 1)
                link(dve.tensor_copy(tmp_i, loc[k]))
                link(dve.tensor_scalar(tmp_i2, tmp_i, LPE - 1, None, ALU.bitwise_and))
                link(dve.tensor_copy(col[:, k, :], tmp_i2))
                link(dve.tensor_tensor(prt[:, k, :], loc[k], col[:, k, :], ALU.subtract))
                link(dve.tensor_scalar(prt[:, k, :], prt[:, k, :], 1.0 / LPE, None, ALU.mult))
                link(dve.tensor_scalar(idx[k], idx[k], float(E), float(LPE), ALU.add, ALU.mult))
                link(dve.tensor_tensor(col[:, k, :], col[:, k, :], idx[k], ALU.add))
                link(dve.tensor_scalar(loc[k], loc[k], float(CAP), None, ALU.is_lt))
                link(dve.tensor_scalar(idx[k], loc[k], -BIG, BIG, ALU.mult, ALU.add))
                link(dve.tensor_tensor(col[:, k, :], col[:, k, :], idx[k], ALU.add))
            dve.wait_ge(setup_act, 3)
            link(dve.tensor_scalar(mx[0], e2, 1.0, None, ALU.add))
            link(dve.reciprocal(mx[1], mx[0]))
            link(dve.tensor_tensor(gates[:, :, 0], mx[1], loc[0], ALU.mult))
            link(dve.tensor_tensor(mx[0], mx[1], e2, ALU.mult))
            dve.tensor_tensor(gates[:, :, 1], mx[0], loc[1], ALU.mult).then_inc(gates_ready, 1)
            prt_f = prt.rearrange("p k i -> p (k i)")
            col_f = col.rearrange("p k i -> p (k i)")
            dve.sem_inc(oh_used, 4)
            with dve.Fori(0, 2 * NT // 4) as i:
                for r in range(4):
                    dve.wait_ge(oh_used, i * 4 + r + 1)
                    dve.tensor_scalar(oh_p[:, r, :], iota[:, 0:P], prt_f[:, bass.ds(i * 4 + r, 1)], None, ALU.is_equal)
                    dve.tensor_scalar(oh_c[:, r, :], iota[:], col_f[:, bass.ds(i * 4 + r, 1)],
                                      tokval[:, bass.ds(i * 4 + r, 1)], ALU.is_equal, ALU.mult).then_inc(oh_ready, 1)
            link(dve.tensor_copy(b2_q, b2_f))
            link(dve.tensor_tensor(b2_r, b2_f, b2_q, ALU.subtract))
            link(dve.tensor_scalar(b2_p[:], b2_q, ident[0:3, 0:1], None, ALU.mult))
            link(dve.tensor_copy(b2_q, b2_r))
            link(dve.tensor_tensor(b2_r, b2_r, b2_q, ALU.subtract))
            link(dve.scalar_tensor_tensor(out=b2_p[:], in0=b2_q, scalar=ident[0:3, 1:2], in1=b2_p[:],
                                          op0=ALU.mult, op1=ALU.add))
            link(dve.tensor_copy(b2_q, b2_r))
            link(dve.scalar_tensor_tensor(out=b2_p[:], in0=b2_q, scalar=ident[0:3, 2:3], in1=b2_p[:],
                                          op0=ALU.mult, op1=ALU.add))
            link(dve.memset(y_sb[:], 0.0))
            dve.wait_ge(oh_used, 2 * NT + 4)
            dst, tok = slot_dst[:, SJ:SJ + E * LPE], slot_tok[:, SJ:SJ + E * LPE]
            link(dve.tensor_scalar(map_f[:], bank[:, 7, 0:E * LPE], -1.0, None, ALU.add))
            link(dve.tensor_scalar(slot_k[:, :, 0], map_f[:], float(T), None, ALU.is_lt))
            link(dve.tensor_scalar(slot_k[:, :, 1], map_f[:], float(T), None, ALU.is_ge))
            link(dve.tensor_scalar(map_g[:], map_f[:], 0.0, 2.0 * T, ALU.is_lt, ALU.mult))
            link(dve.memset(slot_dst[:], 2 * T))
            link(dve.memset(slot_tok[:], 0))
            link(dve.tensor_copy(tok, map_f[:]))
            link(dve.tensor_scalar(tok, tok, T - 1, None, ALU.bitwise_and))
            link(dve.tensor_copy(map_f[:], tok))
            dve.tensor_tensor(dst, map_f[:], map_g[:], ALU.add).then_inc(map_ready, 1)

            dve.sem_inc(scan_done, SCAN0)
            with dve.Fori(0, E) as e:
                with dve.Fori(0, HPE) as hh:
                    with dve.Fori(0, N // NG) as ng:
                        st = (e * HPE + hh) * (N // NG) + ng
                        dve.wait_ge(carry_done, st + 1)
                        for k in range(NG):
                            for dh in range(KD):
                                p = 2 * k + dh
                                dve.wait_ge(a_ready, st * 2 * NG + p + 2)
                                dve.wait_ge(u_ready, st * 2 * NG + p + 2)
                                dve.tensor_tensor_scan(
                                    h[:, p, :], a_ps[dh], u[:, p % 4, :],
                                    carry[:, bass.ds(hh % 2, 1), bass.ds(dh * N + ng * NG + k, 1)]
                                    .rearrange("p a n -> p (a n)"), ALU.mult, ALU.add).then_inc(scan_done, 1)
                            dve.wait_ge(c_ready, st * NG + k + 2)
                            dve.wait_ge(nsum_done, st * NG + k - 1 + NSUM0)
                            for dh in range(KD):
                                p = 2 * k + dh
                                dve.wait_ge(scan_done, st * 2 * NG + p + 1 + SCAN0)
                                dve.tensor_tensor(hc[:, p % 4, :], h[:, p, :], c_ps, ALU.mult).then_inc(hc_done, 1)
                            if k == 1:
                                dve.wait_ge(xg_in, 16 * SJ * (st + 1))
                                dve.wait_ge(evac_done, FP + st * FS + 1)
                                dve.tensor_tensor(gate2[:], xg[:, :, D:D + 2], slot_k[:, bass.ds(st * SJ, SJ), :],
                                                  ALU.mult).then_inc(gate_mul, 1)
                            if k == 2:
                                dve.wait_ge(gate_mul, st + 1)
                                dve.tensor_tensor(gate[:], gate2[:, :, 0], gate2[:, :, 1], ALU.add).then_inc(gate_ready, 1)
                            if k == 3:
                                prep_dt(FP + st, 1 - hh // 2, (hh % 2) * (N // NG) + ng)
                            if k == 6:
                                prep_c(FP + st, 1 - hh // 2, (hh % 2) * (N // NG) + ng)
                        dve.wait_ge(hc_done, (st + 1) * 2 * NG + 1)
                        dve.tensor_copy(carry[:, 1, :].rearrange("p (k n) -> p n k", k=KD)[:, bass.ds(ng * NG, NG), :],
                                        h[:, :, HALF - 1].rearrange("p (n k) -> p n k", k=KD)).then_inc(carry_done, 1)



def kernel(**inputs):
    import numpy as np
    import ml_dtypes
    import concourse.bacc as bacc
    from concourse.bass_utils import run_bass_kernel_spmd

    g = {n: np.asarray(a) for n, a in inputs.items()}
    x = g["L0_attn_x"]
    D = x.shape[2]
    N = g["L0_attn_log_A"].shape[1]
    E, H = g["L0_ffn_b1"].shape
    T = x.shape[0] * x.shape[1]
    lpe = 2 * T // E // P
    sel = np.zeros((96, N, P), ml_dtypes.bfloat16)
    for n in range(N):
        for part in range(3):
            sel[part * 32 + n, n, :] = 1
    arrays = {
        "x": x,
        "log_a": np.concatenate([g["L0_attn_log_A"][:P], g["L0_attn_log_A"][P:]], axis=1),
        "bc_wt": np.concatenate([g["L0_attn_C_w"]] * 3 + [g["L0_attn_B_w"]], axis=0).T,
        "bc_b": np.concatenate([g["L0_attn_C_b"]] * 3 + [g["L0_attn_B_b"]])[:, None],
        "d_skip": g["L0_attn_D_skip"],
        "dt_wt": g["L0_attn_dt_w"].T,
        "dt_b": g["L0_attn_dt_b"].reshape(D // P, P).T,
        "wg": g["L0_ffn_wg"],
        "w1": g["L0_ffn_w1"],
        "b1_t": g["L0_ffn_b1"].reshape(E * H // P, P).T,
        "w2": g["L0_ffn_w2"],
        "b2": g["L0_ffn_b2"].reshape(-1),
        "ident_d": np.eye(P, dtype=np.float32),
        "upper_d": np.triu(np.ones((P, P), np.float32), 1),
        "emin_d": np.tile(np.arange(E, dtype=np.float32) - E, (P, 1)),
        "iota_d": np.tile(np.arange(E * lpe, dtype=np.float32), (P, 1)),
        "tokval_d": (1 + np.arange(2 * T // P, dtype=np.float32)[None, :] * P
                     + np.arange(P, dtype=np.float32)[:, None]),
        "sel_d": sel.reshape(96, N * P),
    }
    arrays = {n: np.ascontiguousarray(a) for n, a in arrays.items()}
    nc = bacc.Bacc("TRN2", target_bir_lowering=False, num_devices=1)
    args = [nc.dram_tensor(n, a.shape, mybir.dt.from_np(a.dtype), kind="ExternalInput").ap() for n, a in arrays.items()]
    out = nc.dram_tensor("out_rows", x.shape, F32, kind="ExternalOutput").ap()
    ssm_moe(nc, *args, out)
    r = run_bass_kernel_spmd(nc, [arrays], core_ids=[0])
    return r.results[0]["out_rows"]
```

```python
from contextlib import ExitStack

import concourse.bass as bass
from concourse import mybir

ALU = mybir.AluOpType
ACT = mybir.ActivationFunctionType
AX = mybir.AxisListType.X
F32 = mybir.dt.float32
BF16 = mybir.dt.bfloat16
I32 = mybir.dt.int32

P = 128
EPS = 1e-5


def ssm_moe(nc, x, log_a, bc_wt, bc_b, d_skip, dt_wt, dt_b, wg, w1, b1_t, w2, b2,
            ident_d, upper_d, emin_d, iota_d, tokval_d, sel_d, out):
    B, S, D = x.shape
    T = B * S
    N = log_a.shape[1] // 2
    E, _, H = w1.shape
    CAP = 2 * T // E
    NT = T // P
    KD = D // P
    HALF = S // 2
    TB = HALF // P
    NG = 8
    HPB = N // NG
    STEPS = B * 2 * HPB
    SPE = STEPS // E
    HPE = SPE // HPB
    G = 4
    U = 4
    NGRP = NT // G
    HC = H // P
    SL = 2 * T // STEPS
    SJ = SL // P
    Q = S // NG
    LPE = CAP // P
    BIG = float(1 << 20)

    xf = x.rearrange("b s d -> (b s) d")
    outf = out.rearrange("b s d -> (b s) d")
    xn_d = nc.dram_tensor("xn_rows", [T, D + 2], F32, kind="Internal").ap()
    xnt_d = nc.dram_tensor("xn_transposed", [KD, P, T], F32, kind="Internal").ap()
    b_d = nc.dram_tensor("b_rows", [2 * N, S], F32, kind="Internal").ap()

    def groups(a):
        return a.rearrange("(i j p) d -> i p j d", p=P, j=G)

    with ExitStack() as ctx:
        def sb(name, shape, dt=F32):
            return ctx.enter_context(nc.sbuf_tensor(name, shape, dt))

        def sem(name):
            return ctx.enter_context(nc.semaphore(name))

        bank = ctx.enter_context(nc.psum_tensor("bank", [P, 8, 512], F32))

        ident = sb("ident", [P, P])
        upper = sb("upper", [P, P])
        ones = sb("ones", [P, P])
        emin = sb("emin", [P, E])
        iota = sb("iota", [P, E * LPE])
        tokval = sb("tokval", [P, 2 * NT])
        sel = sb("sel", [96, N * P], BF16)
        ones3 = sb("ones3", [3, P], BF16)
        zeros3 = sb("zeros3", [3, 512], BF16)
        dskip = sb("dskip", [P, D])
        wg_sb = sb("wg_sb", [P, KD, E])
        a_neg = sb("a_neg", [P, KD * N])
        dtw = sb("dtw", [P, KD, D])
        dtb = sb("dtb", [P, KD])
        bcw = sb("bcw", [P, KD, P])
        bcb = sb("bcb", [P, 1])
        b1_sb = sb("b1_sb", [P, E * HC])
        b2_p = sb("b2_p", [3, E * D], BF16)
        w1_sb = sb("w1_sb", [P, KD, H])
        w2_sb = sb("w2_sb", [P, HC, D])
        h = sb("h", [P, 2 * NG, HALF])
        h_flat = h[:].rearrange("p a t -> p (a t)")
        xt_in, xn = (h_flat[:, i * U * G * D:(i + 1) * U * G * D].rearrange("p (a j d) -> p a j d", a=U, d=D)
                     for i in range(2))
        bstat = sb("bstat", [P, G, 6])
        mv = sb("mv", [P, 2, G, 2])
        rstd = sb("rstd", [P, 2, G])
        eps_c = sb("eps_c", [P, 1])
        b_sb = sb("b_sb", [P, 2, NG, HALF])
        logit, pos, oh0, oh1 = (b_sb[:, 1, 2 * i:2 * i + 2, :].rearrange("p a t -> p (a t)")
                                .rearrange("p (i e) -> p i e", e=E) for i in range(4))
        oh = [oh0, oh1]
        hc = sb("hc", [P, 4, HALF])
        small = iter(hc[:].rearrange("p a (b i) -> p (a b) i", i=NT)[:, n, :] for n in range(4 * HALF // NT))
        mx, idx, loc = ([next(small) for _ in range(2)] for _ in range(3))
        prt, col = (hc[:].rearrange("p a t -> p (a t)")[:, n * NT:(n + 2) * NT] for n in (6, 8))
        prt, col = (t.rearrange("p (k i) -> p k i", k=2) for t in (prt, col))
        e2 = hc[:, 3, HALF - NT:]
        tmp_i, tmp_i2 = (hc[:, 3, n * NT:(n + 1) * NT].bitcast(I32) for n in range(2))
        gates = sb("gates", [P, NT, 2])
        u = sb("u", [P, 4, HALF])
        lt_sb = u[0:E, 0:2, :]
        OHB = 8
        oh_p = u[:].rearrange("p a t -> p (a t)")[:, 0:OHB * P].rearrange("p (r c) -> p r c", r=OHB)
        map_f = sb("map_f", [P, E * LPE])
        map_g = sb("map_g", [P, E * LPE])
        slot_dst = sb("slot_dst", [P, SJ + E * LPE + SJ], I32)
        slot_tok = sb("slot_tok", [P, SJ + E * LPE + SJ], I32)
        slot_k = sb("slot_k", [P, E * LPE, 2])
        xnt = sb("xnt", [P, 2, KD, S])
        dt = sb("dt", [P, 2, KD, S])
        dtx = sb("dtx", [P, 2, KD, S])
        xnt_out = dtx[:, 0].rearrange("p k t -> p (k t)").rearrange("p (a k t) -> p a k t", a=2, k=KD)
        c_p = sb("c_p", [96, 2, S], BF16)
        oh_c = dtx[:, 1].rearrange("p k t -> p (k t)")[:, 0:OHB * E * LPE].rearrange("p (r c) -> p r c", r=OHB)
        carry = sb("carry", [P, 2, KD * N])
        y_sb = sb("y_sb", [P, 2, TB, D])
        b2_f = dt[0:3, 1].rearrange("p k t -> p (k t)")
        b2_r = dtx[0:3, 1].rearrange("p k t -> p (k t)")
        b2_q = hc[0:3].rearrange("p a t -> p (a t)").bitcast(BF16)[:, 0:E * D]
        b2_t = hc[0:3].rearrange("p a t -> p (a t)").bitcast(BF16)[:, E * D:2 * E * D]
        za = sb("za", [P, KD, Q])
        zr = sb("zr", [P, KD, Q])
        ze = sb("ze", [P, KD, Q])
        zl = sb("zl", [P, KD, Q])
        bcv = sb("bcv", [P, Q])
        c_r = sb("c_r", [96, Q])
        gidx = sb("gidx", [P, SJ], I32)
        sidx = sb("sidx", [P, SJ], I32)
        xg = sb("xg", [P, SJ, D + 2])
        gate2 = sb("gate2", [P, SJ, 2])
        gate = sb("gate", [P, SJ])
        xgt = sb("xgt", [P, KD, SL])
        ht = sb("ht", [P, HC, SL])
        o_sb = sb("o_sb", [P, SJ, D])

        y_ps = bank[:, 0:2, :]
        y_blk = y_ps.rearrange("p b (t d) -> p (b t) d", d=D)
        a_ps = [bank[:, 2, :], bank[:, 3, :]]
        c_ps = bank[:, 4, :]
        m_ps = [bank[:, 5, :], bank[:, 6, :]]

        waits_passed = sem("waits_passed")
        consts_in = sem("consts_in")
        weights_in = sem("weights_in")
        x_in = [sem(f"x_in{i}") for i in range(U)]
        stats_done = sem("stats_done")
        aggr_done = sem("aggr_done")
        std_done = sem("std_done")
        rstd_done = sem("rstd_done")
        xn_done = sem("xn_done")
        xn_out = [sem(f"xn_out{i}") for i in range(U)]
        xnt_st = [sem(f"xnt_st{i}") for i in range(2)]
        base_in = [sem(f"base_in{i}") for i in range(U)]
        base_out = [sem(f"base_out{i}") for i in range(U)]
        skip_done = sem("skip_done")
        base_done = sem("base_done")
        turned = sem("turned")
        xnt_done = sem("xnt_done")
        lt_done = sem("lt_done")
        lt_copied = sem("lt_copied")
        logits_done = sem("logits_done")
        dve_seq = sem("dve_seq")
        pool_seq = sem("pool_seq")
        b2_ready = sem("b2_ready")
        pe_route = sem("pe_route")
        gate_in = sem("gate_in")
        gate_out = sem("gate_out")
        oh_ready = sem("oh_ready")
        oh_used = sem("oh_used")
        map_cleared = sem("map_cleared")
        map_ready = sem("map_ready")
        gates_ready = sem("gates_ready")
        gates_out = sem("gates_out")
        setup_act = sem("setup_act")
        setup_dve = sem("setup_dve")
        xnt_in = sem("xnt_in")
        b_in = sem("b_in")
        b_st = sem("b_st")
        w1_in = sem("w1_in")
        w2_in = sem("w2_in")
        xg_in = sem("xg_in")
        gidx_done = sem("gidx_done")
        sidx_done = sem("sidx_done")
        o_scattered = sem("o_scattered")
        fill_done = sem("fill_done")
        evac_done = sem("evac_done")
        c_ready = sem("c_ready")
        a_ready = sem("a_ready")
        u_ready = sem("u_ready")
        scan_done = sem("scan_done")
        hc_done = sem("hc_done")
        nsum_done = sem("nsum_done")
        carry_done = sem("carry_done")
        gate_mul = sem("gate_mul")
        gate_ready = sem("gate_ready")
        y_evac = sem("y_evac")
        y_out = sem("y_out")
        z_done = sem("z_done")
        v_done = sem("v_done")
        l_done = sem("l_done")
        dt_done = sem("dt_done")
        r1_done = sem("r1_done")
        r2_done = sem("r2_done")
        c2_done = sem("c2_done")
        c_parts = sem("c_parts")
        prep_done = sem("prep_done")

        UPS = HC // 2
        FS = UPS + SJ + 2
        TURN = UPS + SJ
        FP = NG + 2
        TURNED0, XNT0, LT0, LOGITS0, YEVAC0, SCAN0, NSUM0 = U, 2, 2, 2, 2, 4, 2
        OHQ = 2 * NT // OHB // NG

        def settle(eng):
            eng.sem_inc(waits_passed, 1)

        def start_at_one(eng, *sems):
            for s in sems:
                eng.sem_inc(s, 1)

        pieces = [(f, 4.0, "up", (f, c)) for f in range(UPS) for c in range(2)]
        for j in range(SJ):
            pieces += [(UPS + j, 2.0, "down", (j, c)) for c in range(HC)] + [(UPS + j, 0.5, "bias", j)]
        total = sum(cost for _, cost, _, _ in pieces)
        first = 1.5
        slices, at = [], 0
        for k in range(NG):
            until = first + k * (total - first) / (NG - 1) + 1.2
            take = []
            while at < len(pieces) and sum(q[1] for q in pieces[:at + 1]) <= until:
                take.append(pieces[at])
                at += 1
            slices.append(take)
        last_of = {q[0]: k for k, take in enumerate(slices) for q in take}
        starts = {next(i for i, q in enumerate(pieces) if q[0] == f) for f in last_of}
        ends = {max(i for i, q in enumerate(pieces) if q[0] == f) for f in last_of}

        block = ctx.enter_context(nc.Block())

        @block.sync
        def _(sp):
            start_at_one(sp, *xn_out, *base_out)
            x_g, xn_g, out_g = groups(xf), groups(xn_d[:, 0:D]), groups(outf)

            def load_x(par, grp):
                sp.dma_start(xt_in[:, par], x_g[bass.ds(grp, 1)].rearrange("a p j d -> (a p) j d")).then_inc(x_in[par], 16)

            load_x(0, 0)
            for dst, src in ((ident, ident_d), (upper, upper_d), (emin, emin_d), (iota, iota_d),
                             (tokval, tokval_d), (sel, sel_d), (dskip, d_skip.partition_broadcast(P)),
                             (wg_sb, wg.rearrange("(k p) e -> p k e", p=P))):
                sp.dma_start(dst[:], src).then_inc(consts_in, 16)
            for r in range(1, U):
                load_x(r, r)
            for dst, src in ((a_neg, log_a), (dtw, dt_wt.rearrange("(k p) e -> p k e", p=P)), (dtb, dt_b),
                             (bcw, bc_wt.rearrange("(k p) e -> p k e", p=P)), (bcb, bc_b),
                             (b1_sb, b1_t), (b2_f, b2.partition_broadcast(3))):
                sp.dma_start(dst if dst is b2_f else dst[:], src).then_inc(weights_in, 16)

            def rows_out(grp, r):
                sp.wait_ge(xn_done, grp + 2)
                sp.dma_start(xn_g[bass.ds(grp, 1)].rearrange("a p j d -> (a p) j d"),
                             xn[:, r]).then_inc(xn_out[r], 16)

            with sp.Fori(0, NGRP // U - 1) as ii:
                for r in range(U):
                    rows_out(ii * U + r, r)
                    load_x(r, ii * U + r + U)
            for r in range(U):
                rows_out(NGRP - U + r, r)
                if r == 0:
                    load_x(0, 0)
            for r in range(2):
                sp.wait_ge(xnt_st[r], 16 * (NGRP // 2) + 1)
            for r in range(U):
                sp.wait_ge(xn_out[r], 16 * (NGRP // U) + 1)
                sp.wait_ge(x_in[r], 16 * (NGRP // U + (r == 0)))

            def load_xnt(par, b):
                src = xnt_d.rearrange("k p t -> p k t")[:, :, bass.ds(b * S, S)]
                sp.dma_start(xnt[:, par], src).then_inc(xnt_in, 16)

            def load_w1(e):
                src = w1[bass.ds(e, 1)].rearrange("a (k p) h -> p (a k) h", p=P)
                sp.dma_start(w1_sb[:], src).then_inc(w1_in, 16)

            def load_w2(e):
                src = w2[bass.ds(e, 1)].rearrange("a (c p) d -> p (a c) d", p=P)
                sp.dma_start(w2_sb[:], src).then_inc(w2_in, 16)

            def load_b(buf, par, th, ng):
                src = b_d[bass.ds(par * N + ng * NG, NG), bass.ds(th * HALF, HALF)].partition_broadcast(P)
                dst = b_sb[:, bass.ds(buf, 1)].rearrange("p a n t -> p (a n) t")
                sp.dma_start(dst, src).then_inc(b_in, 16)

            load_xnt(0, 0)
            sp.wait_ge(xnt_in, 16)
            load_xnt(1, 1)
            load_w1(0)
            load_w2(0)

            def load_base(r, grp):
                for dst, src in ((xt_in, x_g), (xn, xn_g)):
                    sp.dma_start(dst[:, r], src[bass.ds(grp, 1)].rearrange("a p j d -> (a p) j d")).then_inc(base_in[r], 16)

            sp.wait_ge(turned, NGRP + TURNED0)
            for r in range(2):
                load_base(r, r)
            with sp.Fori(0, NGRP // U) as ii:
                for r in range(U):
                    grp, ahead = ii * U + r, (r + 2) % U
                    sp.wait_ge(base_out[ahead], 16 * (ii + (r + 2) // U) + 1)
                    load_base(ahead, (grp + 2) % NGRP)
                    sp.wait_ge(base_done, grp + 1)
                    sp.dma_start(out_g[bass.ds(grp, 1)].rearrange("a p j d -> (a p) j d"),
                                 xn[:, r]).then_inc(base_out[r], 16)
            for r in range(U):
                sp.wait_ge(base_out[r], 16 * (NGRP // U) + 1)
                sp.wait_ge(base_in[r], 32 * (NGRP // U + (r < 2)))
            sp.wait_ge(b_st, 16 * NG + 1)
            load_b(0, 0, 0, 0)
            sp.wait_ge(prep_done, NG + 1)
            sp.wait_ge(xnt_in, 32)
            sp.wait_ge(xg_in, 16 * SJ)
            load_xnt(0, 2)
            sp.wait_ge(map_ready, 1)

            with sp.Fori(0, E) as e:
                with sp.Fori(0, HPE) as hh:
                    with sp.Fori(0, HPB) as ng:
                        st = e * SPE + hh * HPB + ng
                        nx = st + 1
                        sp.wait_ge(u_ready, st * 2 * NG + 1)
                        sp.wait_ge(b_in, 16 * (st + 1))
                        sp.wait_ge(b_st, 16 * (NG + st) + 1)
                        load_b(nx % 2, (nx // NG) % 2, (nx // HPB) % 2, nx % HPB)
                        sp.wait_ge(evac_done, FP + st * FS + 1)
                        settle(sp)
                        sp.dma_start(b_d[bass.ds((1 - hh // 2) * N, N), bass.ds(((hh % 2) * HPB + ng) * Q, Q)],
                                     bcv[96:P, :]).then_inc(b_st, 16)
                    hf = e * HPE + hh
                    sp.wait_ge(prep_done, NG + (hf + 1) * HPB + 1)
                    sp.wait_ge(xnt_in, 16 * (hf + 3))
                    settle(sp)
                    src = xnt_d.rearrange("k p t -> p k t")[:, :, bass.ds((hf // 2 + 3) % B * S + hh % 2 * HALF, HALF)]
                    sp.dma_start(xnt[:, bass.ds(1 - hh // 2, 1), :, bass.ds(hh % 2 * HALF, HALF)]
                                 .rearrange("p a k t -> p (a k) t"), src).then_inc(xnt_in, 16)
                last = FP + (e + 1) * SPE * FS
                sp.wait_ge(fill_done, last - SJ - 2)
                load_w1((e + 1) % E)
                sp.wait_ge(fill_done, last - 2)
                load_w2((e + 1) % E)
            sp.wait_ge(w1_in, 16 * (E + 1))
            sp.wait_ge(w2_in, 16 * (E + 1))
            sp.wait_ge(b_in, 16 * (STEPS + 1))
            sp.wait_ge(b_st, 16 * (NG + STEPS) + 1)
            sp.wait_ge(xnt_in, 16 * (2 * B + 3))
            sp.wait_ge(gates_out, 16)

        @block.tensor
        def _(pe):
            def turn(dst, src, start):
                return pe.matmul(dst, src, ident[:], start=start, stop=True, is_transpose=True, skip_group_check=True)

            start_at_one(pe, c_ready)
            pe.sem_inc(turned, TURNED0)
            pe.sem_inc(logits_done, LOGITS0)
            pe.sem_inc(lt_done, LT0)
            pe.wait_ge(consts_in, 16 * 8)
            lg_ps = bank[:, 4:6, :].rearrange("p b c -> p (b c)")

            def turn_group(grp, r):
                pe.wait_ge(xn_done, grp + 2)
                pe.wait_ge(xnt_done, grp - 1 + XNT0)
                for k in range(KD):
                    for j in range(G):
                        mm = turn(bank[:, 2 * (r % 2) + k, j * P:(j + 1) * P], xn[:, r % U, j, k * P:(k + 1) * P], True)
                mm.then_inc(turned, 1)

            def logits_group(grp, r):
                pe.wait_ge(xnt_done, grp + 1 + XNT0)
                for k in range(KD):
                    mm = pe.matmul(bank[0:E, 6 + r % 2, :], wg_sb[:, k, :], xnt_out[:, r % 2, k, :],
                                   start=(k == 0), stop=(k == KD - 1))
                mm.then_inc(lt_done, 1)

            def turn_logits(grp, r):
                pe.wait_ge(lt_copied, grp + 1)
                for j in range(G):
                    mm = pe.matmul(lg_ps[:, bass.ds((grp * G + j) * E, E)], lt_sb[:, r % 2, j * P:(j + 1) * P],
                                   ident[0:E, 0:E], start=True, stop=True)
                mm.then_inc(logits_done, 1)

            turn_group(0, 0)
            with pe.Fori(0, NGRP // U - 1) as ii:
                for r in range(U):
                    logits_group(ii * U + r, r)
                    turn_group(ii * U + r + 1, r + 1)
                    turn_logits(ii * U + r, r)
            for r in range(U):
                logits_group(NGRP - U + r, r)
                if r < U - 1:
                    turn_group(NGRP - U + r + 1, r + 1)
                turn_logits(NGRP - U + r, r)

            def prep(par, q, f):
                for g in range(3):
                    w = dtw[:, :, g * P:(g + 1) * P] if g < 2 else bcw[:]
                    for k in range(KD):
                        src = xnt[:, bass.ds(par, 1), k, bass.ds(q * Q, Q)].rearrange("p a t -> p (a t)")
                        mm = pe.matmul(m_ps[f][:, g * Q:(g + 1) * Q], w[:, k, :], src, start=(k == 0), stop=(k == KD - 1))
                return mm

            def count(k):
                pe.wait_ge(gate_in, k + 1)
                ohf = oh[k].rearrange("p i e -> p (i e)")
                for c in range(2):
                    pe.matmul(bank[:, c, :], upper[:], ohf[:, c * 512:(c + 1) * 512], start=True, stop=True)
                    mm = pe.matmul(bank[:, 2 + c, :], ones[:], ohf[:, c * 512:(c + 1) * 512], start=True, stop=True)
                mm.then_inc(pe_route, 1)

            for k in range(2):
                count(k)
                if k == 0:
                    pe.wait_ge(gate_out, 1)
            pe.wait_ge(map_cleared, 1)
            pe.wait_ge(gate_out, 1)
            pe.wait_ge(weights_in, 16 * 7)
            pe.wait_ge(xnt_in, 16)
            with pe.Fori(0, NG // 2) as i:
                for f in range(2):
                    pe.wait_ge(evac_done, i * 2 + f + 1)
                    prep(0, i * 2 + f, f).then_inc(fill_done, 1)
                    with pe.Fori(0, OHQ) as o:
                        for r in range(OHB):
                            n = ((i * 2 + f) * OHQ + o) * OHB + r
                            pe.wait_ge(oh_ready, n + 1)
                            pe.matmul(bank[:, 7, 0:E * LPE], oh_p[:, r, :], oh_c[:, r, :], start=False, stop=True,
                                      skip_group_check=True).then_inc(oh_used, 1)
            pe.sem_inc(nsum_done, NSUM0)

            def turn_slots(nx, m):
                pe.wait_ge(xg_in, 16 * SJ * (nx + 1))
                for kk in range(KD):
                    for j in range(SJ):
                        mm = turn(m[:, kk * SL + j * P:kk * SL + (j + 1) * P], xg[:, j, kk * P:(kk + 1) * P], True)
                return mm

            def broadcast_c(nx, state, par, th):
                pe.matmul(c_ps, sel[:, bass.ds(state * P, P)],
                          c_p[:, bass.ds(par, 1), bass.ds(th * HALF, HALF)].rearrange("p a t -> p (a t)"),
                          start=True, stop=True).then_inc(c_ready, 1)

            pe.wait_ge(xnt_in, 32)
            pe.wait_ge(evac_done, NG + 1)
            prep(1, 0, 1)
            pe.wait_ge(c_parts, NG + 1)
            broadcast_c(0, 0, 0, 0)
            turn_slots(0, m_ps[0]).then_inc(fill_done, 2)

            with pe.Fori(0, E) as e:
                with pe.Fori(0, HPE) as hh:
                    hf = e * HPE + hh
                    pe.wait_ge(y_evac, hf + YEVAC0)
                    for c in range(2):
                        pe.matmul(y_ps[:, c, 0:2], ones3[:], zeros3[:, 0:2], start=True, stop=True, skip_group_check=True)
                    with pe.Fori(0, HPB) as ng:
                        st = hf * HPB + ng
                        nx = st + 1
                        for k in range(NG):
                            for piece in slices[k]:
                                f, _, kind, arg = piece
                                at = pieces.index(piece)
                                m = m_ps[f % 2]
                                if at in starts:
                                    pe.wait_ge(evac_done, FP + st * FS + f)
                                if kind == "up":
                                    if arg == (0, 0):
                                        pe.wait_ge(w1_in, 16 * (e + 1))
                                    ch = 2 * arg[0] + arg[1]
                                    for kk in range(KD):
                                        mm = pe.matmul(m[:, arg[1] * SL:(arg[1] + 1) * SL],
                                                       w1_sb[:, kk, ch * P:(ch + 1) * P], xgt[:, kk, :],
                                                       start=(kk == 0), stop=(kk == KD - 1))
                                elif kind == "down":
                                    j, c = arg
                                    if c == 0:
                                        pe.wait_ge(w2_in, 16 * (e + 1))
                                    if j == 0 and c % 2 == 0:
                                        pe.wait_ge(evac_done, FP + st * FS + c // 2 + 2)
                                    mm = pe.matmul(m[:, 0:D], ht[:, c, j * P:(j + 1) * P], w2_sb[:, c, :],
                                                   start=(c == 0), stop=False)
                                else:
                                    mm = pe.matmul(m[:, 0:D], ones3[:], b2_p[:, bass.ds(e * D, D)],
                                                   start=False, stop=True)
                                if at in ends:
                                    mm.then_inc(fill_done, 1)
                            for dh in range(KD):
                                pe.wait_ge(hc_done, st * 2 * NG + 2 * k + dh + 2)
                                if dh == KD - 1:
                                    if k < NG - 1:
                                        broadcast_c(st, ng * NG + k + 1, hh // 2, hh % 2)
                                    else:
                                        pe.wait_ge(c_parts, nx + HPB + 1)
                                        settle(pe)
                                        broadcast_c(nx, nx % HPB * NG, nx // (2 * HPB) % 2, nx // HPB % 2)
                                for tb in range(TB):
                                    mm = turn(y_blk[:, tb, dh * P:(dh + 1) * P],
                                              hc[:, (2 * k + dh) % 4, tb * P:(tb + 1) * P], False)
                            mm.then_inc(nsum_done, 1)
                        pe.wait_ge(evac_done, FP + st * FS + TURN)
                        turn_slots(nx, m_ps[TURN % 2]).then_inc(fill_done, 1)
                        pe.wait_ge(xnt_in, 16 * (nx // NG * 2 + 2))
                        pe.wait_ge(evac_done, FP + st * FS + TURN + 1)
                        settle(pe)
                        prep(1 - nx // NG % 2, nx % NG, (TURN + 1) % 2).then_inc(fill_done, 1)

        @block.scalar
        def _(act):
            start_at_one(act, *xnt_st, evac_done, a_ready, c_parts, b_st)
            act.sem_inc(y_evac, YEVAC0)
            act.sem_inc(xnt_done, XNT0)
            act.wait_ge(setup_dve, 1)
            act.wait_ge(aggr_done, 1)

            def std(par):
                return act.activation(rstd[:, par, :], mv[:, par, :, 1], ACT.Sqrt, bias=eps_c[:, 0:1])

            xnt_g = xnt_d.rearrange("k p (i t) -> i p k t", t=G * P)
            std(0).then_inc(std_done, 1)
            with act.Fori(0, NGRP // U) as ii:
                for r in range(U):
                    grp = ii * U + r
                    act.wait_ge(aggr_done, grp + 2)
                    act.wait_ge(xn_done, grp + 1)
                    std((r + 1) % 2).then_inc(std_done, 1)
                    act.wait_ge(turned, grp + 1 + TURNED0)
                    act.wait_ge(xnt_st[r % 2], 16 * (ii * (U // 2) + r // 2) + 1)
                    act.wait_ge(lt_done, grp - 1 + LT0)
                    act.activation(xnt_out[:, r % 2].rearrange("p k t -> p (k t)"),
                                   bank[:, 2 * (r % 2):2 * (r % 2) + 2, :].rearrange("p b c -> p (b c)"),
                                   ACT.Copy).then_inc(xnt_done, 1)
                    act.wait_ge(xnt_done, grp + 1 + XNT0)
                    act.dma_start(xnt_g[bass.ds(grp, 1)].rearrange("a p k t -> (a p) k t"),
                                  xnt_out[:, r % 2]).then_inc(xnt_st[r % 2], 16)
                    act.wait_ge(lt_done, grp + 1 + LT0)
                    act.wait_ge(logits_done, grp - 1 + LOGITS0)
                    settle(act)
                    act.activation(lt_sb[:, r % 2, :], bank[0:E, 6 + r % 2, :], ACT.Copy).then_inc(lt_copied, 1)

            act.preload_act_table_set("natural_log_exp_and_others")
            act.wait_ge(weights_in, 16 * 7)
            act.activation(a_neg[:], a_neg[:], ACT.Exp).then_inc(setup_act, 1)
            act.wait_ge(setup_act, 1)
            act.mul(a_neg[:], a_neg[:], -1.0).then_inc(setup_act, 1)
            act.wait_ge(gate_in, 3)
            act.activation(e2, e2, ACT.Exp).then_inc(setup_act, 1)
            act.wait_ge(setup_act, 3)

            act.wait_ge(gates_ready, 1)
            act.dma_start(xn_d[:, D:D + 2].rearrange("(i p) d -> p i d", p=P), gates[:]).then_inc(gates_out, 16)

            def evac_prep(m, pdone):
                act.wait_ge(prep_done, pdone + 1)
                for g in range(KD):
                    act.activation(za[:, g, :], m[:, g * Q:(g + 1) * Q], ACT.Abs, bias=dtb[:, g:g + 1])
                for g in range(KD):
                    ins = act.activation(zr[:, g, :], m[:, g * Q:(g + 1) * Q], ACT.Relu, bias=dtb[:, g:g + 1])
                ins.then_inc(z_done, 1)
                act.wait_ge(b_st, 16 * pdone + 1)
                act.activation(bcv[:], m[:, 2 * Q:3 * Q], ACT.Identity, bias=bcb[:, 0:1]).then_inc(evac_done, 1)

            def softplus(pdone, par, q):
                act.wait_ge(z_done, pdone + 1)
                act.activation(ze[:], za[:], ACT.Exp, scale=-1.0).then_inc(v_done, 1)
                act.wait_ge(v_done, pdone + 1)
                c1 = c_p[:, bass.ds(par, 1), bass.ds(q * Q, Q)].rearrange("p a t -> p (a t)")
                act.activation(c1, bcv[0:96, :], ACT.Copy)
                act.activation(zl[:], ze[:], ACT.Ln, bias=1.0).then_inc(l_done, 1)

            def c_part2(pdone, par, q):
                act.wait_ge(r1_done, pdone + 1)
                settle(act)
                for r in (32, 64):
                    ins = act.activation(c_p[r:r + 32, bass.ds(par, 1), bass.ds(q * Q, Q)].rearrange("p a t -> p (a t)"),
                                         c_r[r:r + 32, :], ACT.Copy)
                ins.then_inc(c2_done, 1)

            def c_part3(pdone, par, q):
                act.wait_ge(r2_done, pdone + 1)
                settle(act)
                act.activation(c_p[64:96, bass.ds(par, 1), bass.ds(q * Q, Q)].rearrange("p a t -> p (a t)"),
                               c_r[64:96, :], ACT.Copy).then_inc(c_parts, 1)

            with act.Fori(0, NG // 2) as i:
                for f in range(2):
                    act.wait_ge(fill_done, i * 2 + f + 1)
                    evac_prep(m_ps[f], i * 2 + f)
                    act.wait_ge(evac_done, i * 2 + f + 2)
                    act.dma_start(b_d[0:N, bass.ds((i * 2 + f) * Q, Q)], bcv[96:P, :]).then_inc(b_st, 16)
                    softplus(i * 2 + f, 0, i * 2 + f)
                    c_part2(i * 2 + f, 0, i * 2 + f)
                    c_part3(i * 2 + f, 0, i * 2 + f)

            def decay(dh, state, par, th):
                act.activation(a_ps[dh], dt[:, bass.ds(par, 1), dh, bass.ds(th * HALF, HALF)].rearrange("p a t -> p (a t)"),
                               ACT.Exp, scale=a_neg[:, bass.ds(dh * N + state, 1)]).then_inc(a_ready, 1)

            act.wait_ge(prep_done, NG + 1)
            act.wait_ge(gate_out, 2)
            for dh in range(KD):
                decay(dh, 0, 0, 0)

            with act.Fori(0, E) as e:
                with act.Fori(0, HPE) as hh:
                    hf = e * HPE + hh
                    with act.Fori(0, HPB) as ng:
                        st = hf * HPB + ng
                        nx = st + 1
                        par, q = 1 - hh // 2, (hh % 2) * HPB + ng
                        act.wait_ge(fill_done, FP + st * FS - 1)
                        act.activation(xgt[:].rearrange("p k s -> p (k s)"), m_ps[TURN % 2],
                                       ACT.Copy).then_inc(evac_done, 1)
                        for k in range(NG):
                            if k == NG - 1:
                                act.wait_ge(prep_done, nx + HPB + 1)
                            for dh in range(KD):
                                act.wait_ge(scan_done, st * 2 * NG + 2 * k + dh + 1 + SCAN0)
                                if k < NG - 1:
                                    decay(dh, ng * NG + k + 1, hh // 2, hh % 2)
                                else:
                                    decay(dh, nx % HPB * NG, nx // (2 * HPB) % 2, nx // HPB % 2)
                            if k == 0:
                                act.wait_ge(fill_done, FP + st * FS)
                                evac_prep(m_ps[1], NG + st)
                            if k == 1:
                                softplus(NG + st, par, q)
                            if k == 4:
                                c_part2(NG + st, par, q)
                            for f in sorted(last_of):
                                if last_of[f] != k:
                                    continue
                                m = m_ps[f % 2]
                                if f == UPS - 1:
                                    act.wait_ge(o_scattered, 16 * SJ * (st + 1))
                                if f == UPS:
                                    act.wait_ge(gate_ready, st + 1)
                                act.wait_ge(fill_done, FP + st * FS + f + 1)
                                if f < UPS:
                                    for c in range(2):
                                        ch = 2 * f + c
                                        ins = act.activation(ht[:, ch, :], m[:, c * SL:(c + 1) * SL], ACT.Relu,
                                                             bias=b1_sb[:, bass.ds(e * HC + ch, 1)])
                                    ins.then_inc(evac_done, 1)
                                else:
                                    j = f - UPS
                                    act.activation(o_sb[:, j, :], m[:, 0:D], ACT.Copy,
                                                   scale=gate[:, j:j + 1]).then_inc(evac_done, 1)
                            if k == 6:
                                c_part3(NG + st, par, q)
                    act.wait_ge(nsum_done, (hf + 1) * N + NSUM0)
                    act.wait_ge(y_out, 16 * (hf + 1))
                    act.activation(y_sb[:, bass.ds(hh % 2, 1)].rearrange("p a j d -> p (a j d)"),
                                   y_ps.rearrange("p b c -> p (b c)"), ACT.Copy).then_inc(y_evac, 1)

        @block.gpsimd
        def _(pool):
            start_at_one(pool, u_ready)
            pool.wait_ge(consts_in, 16 * 8)
            dsk = dskip[:].unsqueeze(1).to_broadcast([P, G, D])
            pool.wait_ge(weights_in, 16 * 7)
            seq = [0]

            def link(ins):
                seq[0] += 1
                ins.then_inc(pool_seq, 1)
                pool.wait_ge(pool_seq, seq[0])

            for r in range(3):
                src = b2_f if r == 0 else b2_r
                link(pool.tensor_copy(b2_q, src))
                if r < 2:
                    link(pool.tensor_tensor(b2_r, src, b2_q, ALU.subtract))
                link(pool.tensor_scalar(b2_p[:] if r == 0 else b2_t, b2_q, ident[0:3, r:r + 1], None, ALU.mult))
                if r > 0:
                    link(pool.tensor_tensor(b2_p[:], b2_p[:], b2_t, ALU.add))
            pool.sem_inc(b2_ready, 1)

            with pool.Fori(0, NGRP // U) as ii:
                for r in range(U):
                    pool.wait_ge(base_in[r], 32 * (ii + 1))
                    pool.tensor_tensor(xn[:, r], xn[:, r], dsk, ALU.mult).then_inc(skip_done, 1)
                    pool.wait_ge(skip_done, ii * U + r + 1)
                    pool.tensor_tensor(xn[:, r], xn[:, r], xt_in[:, r], ALU.add).then_inc(base_done, 1)

            def gather(nx):
                pool.wait_ge(gidx_done, nx + 1)
                settle(pool)
                for j in range(SJ):
                    rows = bass.IndirectOffsetOnAxis(ap=gidx[:, j:j + 1], axis=0)
                    pool.indirect_dma_start(xg[:, j, :], None, xn_d, rows,
                                            bounds_check=T - 1, oob_is_err=False).then_inc(xg_in, 16)

            def scatter(st):
                pool.wait_ge(sidx_done, st + 1)
                settle(pool)
                for j in range(SJ):
                    rows = bass.IndirectOffsetOnAxis(ap=sidx[:, j:j + 1], axis=0)
                    pool.indirect_dma_start(outf, rows, o_sb[:, j, :], None, bounds_check=T - 1, oob_is_err=False,
                                            compute_op=ALU.add).then_inc(o_scattered, 16)

            def add_y(hf, buf):
                pool.dma_start(groups(outf)[bass.ds(hf, 1)].rearrange("a p j d -> (a p) j d"),
                               y_sb[:, bass.ds(buf, 1)].rearrange("p a j d -> p (a j) d"), accum_op=ALU.add
                               ).then_inc(y_out, 16)

            pool.wait_ge(gates_out, 16)
            pool.wait_ge(map_ready, 1)
            gather(0)
            pool.wait_ge(map_ready, 2)
            for r in range(U):
                pool.wait_ge(base_out[r], 16 * (NGRP // U) + 1)

            with pool.Fori(0, E) as e:
                with pool.Fori(0, HPE) as hh:
                    hf = e * HPE + hh
                    pool.wait_ge(evac_done, FP + hf * HPB * FS - SJ - 1)
                    pool.wait_ge(y_evac, hf - 1 + YEVAC0)
                    settle(pool)
                    add_y((hf + 2 * B - 2) % (2 * B), hh % 2)
                    pool.wait_ge(prep_done, (hf + 1) * HPB + 1)
                    settle(pool)
                    with pool.Fori(0, HPB) as ng:
                        st = hf * HPB + ng
                        pool.wait_ge(b_in, 16 * (st + 1))
                        for k in range(NG):
                            for dh in range(KD):
                                p = 2 * k + dh
                                pool.wait_ge(scan_done, st * 2 * NG + p - 3 + SCAN0)
                                settle(pool)
                                pool.tensor_tensor(u[:, p % 4, :],
                                                   dtx[:, bass.ds(hh // 2, 1), dh, bass.ds((hh % 2) * HALF, HALF)]
                                                   .rearrange("p a t -> p (a t)"),
                                                   b_sb[:, bass.ds(st % 2, 1), k, :].rearrange("p a t -> p (a t)"),
                                                   ALU.mult).then_inc(u_ready, 1)
                            if k == 2:
                                pool.wait_ge(evac_done, FP + st * FS - 1)
                                pool.wait_ge(y_out, 16 * (hf + 1))
                                scatter(st)
                            if k == 4:
                                pool.wait_ge(fill_done, FP + st * FS - 1)
                                pool.wait_ge(gate_ready, st + 1)
                                gather(st + 1)
            pool.wait_ge(evac_done, FP + STEPS * FS - 1)
            scatter(STEPS)
            pool.wait_ge(o_scattered, 16 * SJ * (STEPS + 1))
            for n in range(2):
                pool.wait_ge(y_evac, 2 * B - 1 + n + YEVAC0)
                add_y(2 * B - 2 + n, n)
                pool.wait_ge(y_out, 16 * (2 * B + 1 + n))
            pool.wait_ge(xg_in, 16 * SJ * (STEPS + 1))

        @block.vector
        def _(dve):
            start_at_one(dve, xn_done, hc_done, carry_done, prep_done)
            seq = [0]

            def link(ins):
                seq[0] += 1
                ins.then_inc(dve_seq, 1)
                dve.wait_ge(dve_seq, seq[0])

            dve.memset(eps_c[:], EPS)
            dve.memset(ones[:], 1.0)
            dve.memset(ones3[:], 1.0)
            dve.memset(carry[:], 0.0)
            dve.memset(o_sb[:], 0.0)
            dve.memset(y_sb[:], 0.0)
            dve.memset(slot_dst[:], 2 * T)
            dve.memset(slot_tok[:], 0)
            dve.memset(zeros3[:], 0.0).then_inc(setup_dve, 1)
            dve.wait_ge(setup_dve, 1)
            def stats(par):
                for j in range(G):
                    ins = dve.bn_stats(bstat[:, j, :], xt_in[:, par, j, :])
                return ins

            def aggr(par):
                for j in range(G):
                    ins = dve.bn_aggr(mv[:, par, j, :], bstat[:, j, :])
                return ins

            dve.wait_ge(x_in[0], 16)
            stats(0).then_inc(stats_done, 1)
            dve.wait_ge(stats_done, 1)
            aggr(0).then_inc(aggr_done, 1)
            with dve.Fori(0, NGRP // U) as ii:
                for r in range(U):
                    grp, s2 = ii * U + r, r % 2
                    dve.wait_ge(x_in[(r + 1) % U], 16 * (ii + 1 + (r + 1) // U))
                    dve.wait_ge(aggr_done, grp + 1)
                    stats((r + 1) % U).then_inc(stats_done, 1)
                    dve.wait_ge(stats_done, grp + 2)
                    settle(dve)
                    dve.wait_ge(xn_done, grp + 1)
                    settle(dve)
                    aggr(1 - s2).then_inc(aggr_done, 1)
                    dve.wait_ge(std_done, grp + 1)
                    dve.reciprocal(rstd[:, s2, :], rstd[:, s2, :]).then_inc(rstd_done, 1)
                    dve.wait_ge(rstd_done, grp + 1)
                    dve.wait_ge(xn_out[r], 16 * ii + 1)
                    dve.wait_ge(turned, grp - U + 1 + TURNED0)
                    for j in range(G):
                        ins = dve.tensor_scalar(xn[:, r, j, :], xt_in[:, r, j, :], mv[:, s2, j, 0:1],
                                                rstd[:, s2, j:j + 1], ALU.subtract, ALU.mult)
                    ins.then_inc(xn_done, 1)

            dve.wait_ge(b2_ready, 1)
            dve.wait_ge(logits_done, NGRP + LOGITS0)
            dve.wait_ge(consts_in, 16 * 8)
            link(dve.tensor_copy(logit.rearrange("p i e -> p (i e)"), bank[:, 4:6, :].rearrange("p b c -> p (b c)")))
            dve.memset(bank[:, 7, 0:E * LPE], 0.0).then_inc(map_cleared, 1)
            per_e = lambda t: t.unsqueeze(1).to_broadcast([P, NT, E])
            per_i = lambda t: t.unsqueeze(2).to_broadcast([P, NT, E])
            for k in range(2):
                link(dve.tensor_reduce(mx[k], logit, AX, ALU.max))
                link(dve.tensor_tensor(pos, logit, per_i(mx[k]), ALU.is_equal))
                link(dve.tensor_tensor(pos, pos, per_e(emin[:]), ALU.mult))
                link(dve.tensor_reduce(idx[k], pos, AX, ALU.min))
                link(dve.tensor_tensor(oh[k], per_e(emin[:]), per_i(idx[k]), ALU.is_equal))
                if k == 0:
                    link(dve.scalar_tensor_tensor(out=logit, in0=oh[0], scalar=-3.0e38, in1=logit,
                                                  op0=ALU.mult, op1=ALU.add))
                dve.sem_inc(gate_in, 1)
            dve.tensor_tensor(e2, mx[1], mx[0], ALU.subtract).then_inc(gate_in, 1)

            def prep_dt(pdone, par, q):
                dst = lambda t: t[:, bass.ds(par, 1), :, bass.ds(q * Q, Q)].rearrange("p a k t -> p (a k) t")
                dve.wait_ge(l_done, pdone + 1)
                dve.tensor_tensor(dst(dt), zr[:], zl[:], ALU.add).then_inc(dt_done, 1)
                dve.wait_ge(c_parts, pdone + 1)
                c_all = c_p[:, bass.ds(par, 1), bass.ds(q * Q, Q)].rearrange("p a t -> p (a t)")
                dve.tensor_tensor(c_r[:], bcv[0:96, :], c_all, ALU.subtract).then_inc(r1_done, 1)
                dve.wait_ge(dt_done, pdone + 1)
                dve.tensor_tensor(dst(dtx), dst(dt), dst(xnt), ALU.mult).then_inc(prep_done, 1)

            def prep_c(pdone, par, q):
                dve.wait_ge(c2_done, pdone + 1)
                c_all = c_p[:, bass.ds(par, 1), bass.ds(q * Q, Q)].rearrange("p a t -> p (a t)")
                dve.tensor_tensor(c_r[:], c_r[:], c_all, ALU.subtract).then_inc(r2_done, 1)


            tot = bank[:, 2:4, :].rearrange("p b c -> p (b c)").rearrange("p (i e) -> p i e", e=E)
            before = bank[:, 0:2, :].rearrange("p b c -> p (b c)").rearrange("p (i e) -> p i e", e=E)
            for k in range(2):
                dve.wait_ge(pe_route, k + 1)
                for ee in range(E):
                    init = 0.0 if k == 0 else map_g[:, ee:ee + 1]
                    ins = dve.tensor_tensor_scan(pos[:, :, ee], ones[:, 0:NT], tot[:, :, ee], init, ALU.mult, ALU.add)
                link(ins)
                if k == 0:
                    dve.tensor_copy(map_g[:, 0:E], pos[:, NT - 1, :])
                link(dve.tensor_tensor(logit, pos, tot, ALU.subtract))
                link(dve.tensor_tensor(logit, logit, before, ALU.add))
                link(dve.tensor_tensor(logit, logit, oh[k], ALU.mult))
                link(dve.tensor_reduce(loc[k], logit, AX, ALU.add))
                dve.sem_inc(gate_out, 1)
                link(dve.tensor_copy(tmp_i, loc[k]))
                link(dve.tensor_scalar(tmp_i2, tmp_i, LPE - 1, None, ALU.bitwise_and))
                link(dve.tensor_copy(col[:, k, :], tmp_i2))
                link(dve.tensor_tensor(prt[:, k, :], loc[k], col[:, k, :], ALU.subtract))
                link(dve.tensor_scalar(prt[:, k, :], prt[:, k, :], 1.0 / LPE, None, ALU.mult))
                link(dve.tensor_scalar(idx[k], idx[k], float(E), float(LPE), ALU.add, ALU.mult))
                link(dve.tensor_tensor(col[:, k, :], col[:, k, :], idx[k], ALU.add))
                link(dve.tensor_scalar(loc[k], loc[k], float(CAP), None, ALU.is_lt))
                link(dve.tensor_scalar(idx[k], loc[k], -BIG, BIG, ALU.mult, ALU.add))
                link(dve.tensor_tensor(col[:, k, :], col[:, k, :], idx[k], ALU.add))
            dve.wait_ge(setup_act, 3)
            link(dve.tensor_scalar(mx[0], e2, 1.0, None, ALU.add))
            link(dve.reciprocal(mx[1], mx[0]))
            link(dve.tensor_tensor(gates[:, :, 0], mx[1], loc[0], ALU.mult))
            link(dve.tensor_tensor(mx[0], mx[1], e2, ALU.mult))
            dve.tensor_tensor(gates[:, :, 1], mx[0], loc[1], ALU.mult).then_inc(gates_ready, 1)
            prt_f = prt.rearrange("p k i -> p (k i)")
            col_f = col.rearrange("p k i -> p (k i)")
            dve.sem_inc(oh_used, OHB)
            with dve.Fori(0, NG) as q:
                with dve.Fori(0, OHQ) as o:
                    for r in range(OHB):
                        i = (q * OHQ + o) * OHB + r
                        if r % (OHB // 2) == 0:
                            dve.wait_ge(oh_used, i + OHB // 2)
                            dve.tensor_tensor(oh_p[:, r:r + OHB // 2, :],
                                              iota[:, 0:P].unsqueeze(1).to_broadcast([P, OHB // 2, P]),
                                              prt_f[:, bass.ds(i, OHB // 2)].unsqueeze(2)
                                              .to_broadcast([P, OHB // 2, P]), ALU.is_equal)
                        dve.tensor_scalar(oh_c[:, r, :], iota[:], col_f[:, bass.ds(i, 1)],
                                          tokval[:, bass.ds(i, 1)], ALU.is_equal, ALU.mult).then_inc(oh_ready, 1)
                prep_dt(q, 0, q)
                prep_c(q, 0, q)
            dve.wait_ge(oh_used, 2 * NT + OHB)
            dst, tok = slot_dst[:, SJ:SJ + E * LPE], slot_tok[:, SJ:SJ + E * LPE]
            link(dve.tensor_scalar(map_f[:], bank[:, 7, 0:E * LPE], -1.0, None, ALU.add))
            link(dve.tensor_copy(tok, map_f[:]))
            dve.tensor_scalar(tok, tok, T - 1, None, ALU.bitwise_and).then_inc(map_ready, 1)
            dve.wait_ge(map_ready, 1)
            dve.tensor_copy(gidx[:], slot_tok[:, SJ:2 * SJ]).then_inc(gidx_done, 1)
            dve.tensor_scalar(slot_k[:, :, 0], map_f[:], float(T), None, ALU.is_lt)
            dve.tensor_scalar(slot_k[:, :, 1], map_f[:], float(T), None, ALU.is_ge)
            link(dve.tensor_scalar(map_g[:], map_f[:], 0.0, 2.0 * T, ALU.is_lt, ALU.mult))
            link(dve.tensor_copy(map_f[:], tok))
            dve.tensor_tensor(dst, map_f[:], map_g[:], ALU.add).then_inc(map_ready, 1)
            dve.wait_ge(map_ready, 2)

            def lay_gather(nx):
                dve.tensor_copy(gidx[:], slot_tok[:, bass.ds(nx * SJ + SJ, SJ)]).then_inc(gidx_done, 1)

            def lay_scatter(st):
                dve.wait_ge(evac_done, FP + st * FS - SJ - 1)
                dve.tensor_copy(sidx[:], slot_dst[:, bass.ds(st * SJ, SJ)]).then_inc(sidx_done, 1)

            dve.sem_inc(scan_done, SCAN0)
            with dve.Fori(0, E) as e:
                with dve.Fori(0, HPE) as hh:
                    with dve.Fori(0, HPB) as ng:
                        st = (e * HPE + hh) * HPB + ng
                        dve.wait_ge(carry_done, st + 1)
                        for k in range(NG):
                            for dh in range(KD):
                                p = 2 * k + dh
                                dve.wait_ge(a_ready, st * 2 * NG + p + 2)
                                dve.wait_ge(u_ready, st * 2 * NG + p + 2)
                                dve.tensor_tensor_scan(
                                    h[:, p, :], a_ps[dh], u[:, p % 4, :],
                                    carry[:, bass.ds(hh % 2, 1), bass.ds(dh * N + ng * NG + k, 1)]
                                    .rearrange("p a n -> p (a n)"), ALU.mult, ALU.add).then_inc(scan_done, 1)
                            dve.wait_ge(c_ready, st * NG + k + 2)
                            dve.wait_ge(nsum_done, st * NG + k - 1 + NSUM0)
                            for dh in range(KD):
                                p = 2 * k + dh
                                dve.wait_ge(scan_done, st * 2 * NG + p + 1 + SCAN0)
                                dve.tensor_tensor(hc[:, p % 4, :], h[:, p, :], c_ps, ALU.mult).then_inc(hc_done, 1)
                            if k == 0:
                                lay_scatter(st)
                            if k == 1:
                                dve.wait_ge(xg_in, 16 * SJ * (st + 1))
                                dve.wait_ge(evac_done, FP + st * FS - 1)
                                dve.tensor_tensor(gate2[:], xg[:, :, D:D + 2], slot_k[:, bass.ds(st * SJ, SJ), :],
                                                  ALU.mult).then_inc(gate_mul, 1)
                                lay_gather(st + 1)
                            if k == 2:
                                dve.wait_ge(gate_mul, st + 1)
                                dve.tensor_tensor(gate[:], gate2[:, :, 0], gate2[:, :, 1], ALU.add).then_inc(gate_ready, 1)
                            if k == 3:
                                prep_dt(NG + st, 1 - hh // 2, (hh % 2) * HPB + ng)
                            if k == 5:
                                prep_c(NG + st, 1 - hh // 2, (hh % 2) * HPB + ng)
                        dve.wait_ge(scan_done, (st + 1) * 2 * NG + SCAN0)
                        dve.tensor_copy(carry[:, 1, :].rearrange("p (k n) -> p n k", k=KD)[:, bass.ds(ng * NG, NG), :],
                                        h[:, :, HALF - 1].rearrange("p (n k) -> p n k", k=KD)).then_inc(carry_done, 1)
            lay_scatter(STEPS)



def kernel(**inputs):
    import numpy as np
    import ml_dtypes
    import concourse.bacc as bacc
    from concourse.bass_utils import run_bass_kernel_spmd

    g = {n: np.asarray(a) for n, a in inputs.items()}
    x = g["L0_attn_x"]
    D = x.shape[2]
    N = g["L0_attn_log_A"].shape[1]
    E, H = g["L0_ffn_b1"].shape
    T = x.shape[0] * x.shape[1]
    lpe = 2 * T // E // P
    sel = np.zeros((96, N, P), ml_dtypes.bfloat16)
    for n in range(N):
        for part in range(3):
            sel[part * 32 + n, n, :] = 1
    arrays = {
        "x": x,
        "log_a": np.concatenate([g["L0_attn_log_A"][:P], g["L0_attn_log_A"][P:]], axis=1),
        "bc_wt": np.concatenate([g["L0_attn_C_w"]] * 3 + [g["L0_attn_B_w"]], axis=0).T,
        "bc_b": np.concatenate([g["L0_attn_C_b"]] * 3 + [g["L0_attn_B_b"]])[:, None],
        "d_skip": g["L0_attn_D_skip"],
        "dt_wt": g["L0_attn_dt_w"].T,
        "dt_b": g["L0_attn_dt_b"].reshape(D // P, P).T,
        "wg": g["L0_ffn_wg"],
        "w1": g["L0_ffn_w1"],
        "b1_t": g["L0_ffn_b1"].reshape(E * H // P, P).T,
        "w2": g["L0_ffn_w2"],
        "b2": g["L0_ffn_b2"].reshape(-1),
        "ident_d": np.eye(P, dtype=np.float32),
        "upper_d": np.triu(np.ones((P, P), np.float32), 1),
        "emin_d": np.tile(np.arange(E, dtype=np.float32) - E, (P, 1)),
        "iota_d": np.tile(np.arange(E * lpe, dtype=np.float32), (P, 1)),
        "tokval_d": (1 + np.arange(2 * T // P, dtype=np.float32)[None, :] * P
                     + np.arange(P, dtype=np.float32)[:, None]),
        "sel_d": sel.reshape(96, N * P),
    }
    arrays = {n: np.ascontiguousarray(a) for n, a in arrays.items()}
    nc = bacc.Bacc("TRN2", target_bir_lowering=False, num_devices=1)
    args = [nc.dram_tensor(n, a.shape, mybir.dt.from_np(a.dtype), kind="ExternalInput").ap() for n, a in arrays.items()]
    out = nc.dram_tensor("out_rows", x.shape, F32, kind="ExternalOutput").ap()
    ssm_moe(nc, *args, out)
    r = run_bass_kernel_spmd(nc, [arrays], core_ids=[0])
    return r.results[0]["out_rows"]
```
